# Optimizing a Trainium2 kernel written in Bass

```python
import numpy as np
import jax
import jax.numpy as jnp

def _softmax(x, axis=-1):
    return jax.nn.softmax(x, axis=axis)

def _gelu(x):
    return jax.nn.gelu(x, approximate=True)

def _silu(x):
    return jax.nn.silu(x)

def _sigmoid(x):
    return jax.nn.sigmoid(x)

def _layernorm(x, axis=-1, eps=1e-05):
    m = jnp.mean(x, axis=axis, keepdims=True)
    v = jnp.var(x, axis=axis, keepdims=True)
    return (x - m) / jnp.sqrt(v + eps)

def _scatter_add(tgt, idx, src, axis=0):
    return tgt.at[idx].add(src)

def _segment_sum(src, seg, n):
    return jax.ops.segment_sum(src, seg, n)
kernel_name = 'mk_seq_postln_d2_jaxref_r8_9a316b'

def setup_inputs(seed: int=0):
    np.random.seed(seed)
    _w = jnp.asarray

    def _L0_attn_setup():
        import jax, jax.numpy as jnp
        import numpy as np
        B, S, D = (2, 256, 128)
        H, P = (16, 64)
        NUM_OUT = 128
        key = jax.random.key(seed)
        ks = jax.random.split(key, 9)
        sc = 0.05
        return {'x': jax.random.normal(ks[0], (B, S, D), jnp.float32), 'q_w': jax.random.normal(ks[1], (H, P, D), jnp.float32) * sc, 'q_b': jax.random.normal(ks[2], (H, 1, P), jnp.float32) * sc, 'k_w': jax.random.normal(ks[3], (H, P, D), jnp.float32) * sc, 'k_b': jax.random.normal(ks[4], (H, 1, P), jnp.float32) * sc, 'v_w': jax.random.normal(ks[5], (H, P, D), jnp.float32) * sc, 'v_b': jax.random.normal(ks[6], (H, 1, P), jnp.float32) * sc, 'l_w': jax.random.normal(ks[7], (NUM_OUT, P * H), jnp.float32) * sc, 'l_b': jax.random.normal(ks[8], (1, NUM_OUT), jnp.float32) * sc}
    _L0_attn_in = _L0_attn_setup()

    def _L0_ffn_setup():
        import jax, jax.numpy as jnp
        import numpy as np
        H = 128
        I = 88
        E = 64
        TOP_K = 8
        NG = 8
        TOPK_GROUP = 4
        N_SHARED = 2
        ROUTED_SCALE = 2.5
        S_I = I * N_SHARED

        def _route(x, gate_w, gate_bias):
            T = x.shape[0]
            logits = x @ gate_w.T
            scores = jax.nn.sigmoid(logits)
            scores_for_choice = scores + gate_bias[None, :]
            grp = scores_for_choice.reshape(T, NG, E // NG)
            group_scores = jnp.sum(jax.lax.top_k(grp, 2)[0], axis=-1)
            _, gidx = jax.lax.top_k(group_scores, TOPK_GROUP)
            gmask = jnp.zeros((T, NG), dtype=scores.dtype).at[jnp.arange(T)[:, None], gidx].set(1.0)
            emask = jnp.repeat(gmask, E // NG, axis=1)
            masked = jnp.where(emask > 0, scores_for_choice, 0.0)
            _, topk_idx = jax.lax.top_k(masked, TOP_K)
            topk_w = jnp.take_along_axis(scores, topk_idx, axis=1)
            topk_w = topk_w / (jnp.sum(topk_w, axis=-1, keepdims=True) + 1e-20)
            topk_w = topk_w * ROUTED_SCALE
            rw = jnp.zeros((T, E), dtype=scores.dtype).at[jnp.arange(T)[:, None], topk_idx].add(topk_w)
            return rw

        def _mlp(x, gw, uw, dw):
            return jax.nn.silu(x @ gw.T) * (x @ uw.T) @ dw.T
        key = jax.random.key(seed)
        ks = jax.random.split(key, 10)
        sc = 0.02
        return {'hidden_states': jax.random.normal(ks[0], (1, 128, H), dtype=jnp.float32), 'gate_w': sc * jax.random.normal(ks[1], (E, H), dtype=jnp.float32), 'gate_bias': sc * jax.random.normal(ks[2], (E,), dtype=jnp.float32), 'Wg': sc * jax.random.normal(ks[3], (E, I, H), dtype=jnp.float32), 'Wu': sc * jax.random.normal(ks[4], (E, I, H), dtype=jnp.float32), 'Wd': sc * jax.random.normal(ks[5], (E, H, I), dtype=jnp.float32), 'Sg': sc * jax.random.normal(ks[6], (S_I, H), dtype=jnp.float32), 'Su': sc * jax.random.normal(ks[7], (S_I, H), dtype=jnp.float32), 'Sd': sc * jax.random.normal(ks[8], (H, S_I), dtype=jnp.float32)}
    _L0_ffn_in = _L0_ffn_setup()

    def _L1_attn_setup():
        import jax, jax.numpy as jnp
        import numpy as np
        MODEL_DIM = 128
        NUM_HEADS = 16
        D_K = MODEL_DIM // NUM_HEADS
        MAX_SEQ_LEN = 512

        def _xavier(key, shape):
            fan_in, fan_out = (shape[1], shape[0])
            limit = np.sqrt(6.0 / (fan_in + fan_out)).astype(np.float32)
            return jax.random.uniform(key, shape, jnp.float32, -limit, limit)
        key = jax.random.key(seed)
        ks = jax.random.split(key, 6)
        x = jax.random.normal(ks[0], (2, 256, MODEL_DIM), jnp.float32)
        wq = _xavier(ks[1], (MODEL_DIM, MODEL_DIM))
        wk = _xavier(ks[2], (MODEL_DIM, MODEL_DIM))
        wv = _xavier(ks[3], (MODEL_DIM, MODEL_DIM))
        wo = _xavier(ks[4], (MODEL_DIM, MODEL_DIM))
        bq = jnp.zeros((MODEL_DIM,), jnp.float32)
        bk = jnp.zeros((MODEL_DIM,), jnp.float32)
        bv = jnp.zeros((MODEL_DIM,), jnp.float32)
        bo = jnp.zeros((MODEL_DIM,), jnp.float32)
        half = D_K // 2
        theta = jnp.power(10000.0, jnp.arange(half, dtype=jnp.float32) * (-2.0 / D_K))
        angles = jnp.arange(MAX_SEQ_LEN, dtype=jnp.float32)[:, None] * theta[None, :]
        rot_cos = jnp.cos(angles)
        rot_sin = jnp.sin(angles)
        return {'x': x, 'wq': wq, 'bq': bq, 'wk': wk, 'bk': bk, 'wv': wv, 'bv': bv, 'wo': wo, 'bo': bo, 'rot_cos': rot_cos, 'rot_sin': rot_sin}
    _L1_attn_in = _L1_attn_setup()

    def _L1_ffn_setup():
        import jax, jax.numpy as jnp
        import numpy as np
        B, S, K, N = (8, 1024, 128, 128)
        key = jax.random.key(seed)
        k1, k2, k3, k4 = jax.random.split(key, 4)
        x = jax.random.normal(k1, (B, S, K), dtype=jnp.float32)
        CB = jnp.clip(jnp.round(jax.random.normal(k2, (N, K), dtype=jnp.float32) * 42.0), -127.0, 127.0)
        SCB = jax.random.uniform(k3, (N,), dtype=jnp.float32, minval=0.5, maxval=2.0)
        bias = jax.random.normal(k4, (N,), dtype=jnp.float32) * 0.02
        return {'x': x, 'CB': CB, 'SCB': SCB, 'bias': bias}
    _L1_ffn_in = _L1_ffn_setup()
    _d = {'L0_attn_x': _L0_attn_in['x'], 'L0_attn_q_w': _L0_attn_in['q_w'], 'L0_attn_q_b': _L0_attn_in['q_b'], 'L0_attn_k_w': _L0_attn_in['k_w'], 'L0_attn_k_b': _L0_attn_in['k_b'], 'L0_attn_v_w': _L0_attn_in['v_w'], 'L0_attn_v_b': _L0_attn_in['v_b'], 'L0_attn_l_w': _L0_attn_in['l_w'], 'L0_attn_l_b': _L0_attn_in['l_b'], 'L0_ffn_gate_w': _L0_ffn_in['gate_w'], 'L0_ffn_gate_bias': _L0_ffn_in['gate_bias'], 'L0_ffn_Wg': _L0_ffn_in['Wg'], 'L0_ffn_Wu': _L0_ffn_in['Wu'], 'L0_ffn_Wd': _L0_ffn_in['Wd'], 'L0_ffn_Sg': _L0_ffn_in['Sg'], 'L0_ffn_Su': _L0_ffn_in['Su'], 'L0_ffn_Sd': _L0_ffn_in['Sd'], 'L1_attn_wq': _L1_attn_in['wq'], 'L1_attn_bq': _L1_attn_in['bq'], 'L1_attn_wk': _L1_attn_in['wk'], 'L1_attn_bk': _L1_attn_in['bk'], 'L1_attn_wv': _L1_attn_in['wv'], 'L1_attn_bv': _L1_attn_in['bv'], 'L1_attn_wo': _L1_attn_in['wo'], 'L1_attn_bo': _L1_attn_in['bo'], 'L1_attn_rot_cos': _L1_attn_in['rot_cos'], 'L1_attn_rot_sin': _L1_attn_in['rot_sin'], 'L1_ffn_CB': _L1_ffn_in['CB'], 'L1_ffn_SCB': _L1_ffn_in['SCB'], 'L1_ffn_bias': _L1_ffn_in['bias']}
    _x0 = _d['L0_attn_x']
    _d['L0_attn_x'] = jax.random.normal(jax.random.fold_in(jax.random.key(seed), 1), (16, 256, 128), dtype=_x0.dtype)
    del _x0
    return _d

def reference(L0_attn_x, L0_attn_q_w, L0_attn_q_b, L0_attn_k_w, L0_attn_k_b, L0_attn_v_w, L0_attn_v_b, L0_attn_l_w, L0_attn_l_b, L0_ffn_gate_w, L0_ffn_gate_bias, L0_ffn_Wg, L0_ffn_Wu, L0_ffn_Wd, L0_ffn_Sg, L0_ffn_Su, L0_ffn_Sd, L1_attn_wq, L1_attn_bq, L1_attn_wk, L1_attn_bk, L1_attn_wv, L1_attn_bv, L1_attn_wo, L1_attn_bo, L1_attn_rot_cos, L1_attn_rot_sin, L1_ffn_CB, L1_ffn_SCB, L1_ffn_bias):

    def _L0_attn_ref(x, q_w, q_b, k_w, k_b, v_w, v_b, l_w, l_b):
        import jax, jax.numpy as jnp
        import numpy as np
        B, S, D = (2, 256, 128)
        H, P = (16, 64)
        NUM_OUT = 128
        q = jnp.einsum('bsd,hpd->bhsp', x, q_w) + q_b
        k = jnp.einsum('bsd,hpd->bhsp', x, k_w) + k_b
        v = jnp.einsum('bsd,hpd->bhsp', x, v_w) + v_b
        scores = jnp.einsum('bhqp,bhkp->bhqk', q, k) / jnp.sqrt(jnp.float32(P))
        attn = jax.nn.softmax(scores, axis=2)
        ctx = jnp.einsum('bhqk,bhkp->bqhp', attn, v)
        concat = ctx.reshape(ctx.shape[0], ctx.shape[1], H * P)
        out = concat @ l_w.T + l_b
        return out

    def _L0_ffn_ref(hidden_states, gate_w, gate_bias, Wg, Wu, Wd, Sg, Su, Sd):
        import jax, jax.numpy as jnp
        import numpy as np
        H = 128
        I = 88
        E = 64
        TOP_K = 8
        NG = 8
        TOPK_GROUP = 4
        N_SHARED = 2
        ROUTED_SCALE = 2.5
        S_I = I * N_SHARED

        def _route(x, gate_w, gate_bias):
            T = x.shape[0]
            logits = x @ gate_w.T
            scores = jax.nn.sigmoid(logits)
            scores_for_choice = scores + gate_bias[None, :]
            grp = scores_for_choice.reshape(T, NG, E // NG)
            group_scores = jnp.sum(jax.lax.top_k(grp, 2)[0], axis=-1)
            _, gidx = jax.lax.top_k(group_scores, TOPK_GROUP)
            gmask = jnp.zeros((T, NG), dtype=scores.dtype).at[jnp.arange(T)[:, None], gidx].set(1.0)
            emask = jnp.repeat(gmask, E // NG, axis=1)
            masked = jnp.where(emask > 0, scores_for_choice, 0.0)
            _, topk_idx = jax.lax.top_k(masked, TOP_K)
            topk_w = jnp.take_along_axis(scores, topk_idx, axis=1)
            topk_w = topk_w / (jnp.sum(topk_w, axis=-1, keepdims=True) + 1e-20)
            topk_w = topk_w * ROUTED_SCALE
            rw = jnp.zeros((T, E), dtype=scores.dtype).at[jnp.arange(T)[:, None], topk_idx].add(topk_w)
            return rw

        def _mlp(x, gw, uw, dw):
            return jax.nn.silu(x @ gw.T) * (x @ uw.T) @ dw.T
        B, S, _ = hidden_states.shape
        x = hidden_states.reshape(B * S, H)
        rw = _route(x, gate_w, gate_bias)
        expert_out = jax.vmap(lambda gw_, uw_, dw_: _mlp(x, gw_, uw_, dw_))(Wg, Wu, Wd)
        routed = jnp.einsum('eth,te->th', expert_out, rw)
        shared = _mlp(x, Sg, Su, Sd)
        out = (routed + shared).reshape(B, S, H)
        return out

    def _L1_attn_ref(x, wq, bq, wk, bk, wv, bv, wo, bo, rot_cos, rot_sin):
        import jax, jax.numpy as jnp
        import numpy as np
        MODEL_DIM = 128
        NUM_HEADS = 16
        D_K = MODEL_DIM // NUM_HEADS
        MAX_SEQ_LEN = 512

        def _xavier(key, shape):
            fan_in, fan_out = (shape[1], shape[0])
            limit = np.sqrt(6.0 / (fan_in + fan_out)).astype(np.float32)
            return jax.random.uniform(key, shape, jnp.float32, -limit, limit)
        b, t, m = x.shape
        h, d = (NUM_HEADS, m // NUM_HEADS)
        q = (x @ wq.T + bq).reshape(b, h, t, d)
        k = (x @ wk.T + bk).reshape(b, h, t, d)
        v = (x @ wv.T + bv).reshape(b, h, t, d)
        c = rot_cos[t]
        s = rot_sin[t]

        def rope(u):
            ur = u.reshape(b, h, t, d // 2, 2)
            re, im = (ur[..., 0], ur[..., 1])
            return jnp.stack([re * c - im * s, re * s + im * c], axis=-1).reshape(b, h, t, d)
        q, k = (rope(q), rope(k))
        scores = jnp.einsum('bhqd,bhkd->bhqk', q, k) / np.float32(np.sqrt(d))
        p = jax.nn.softmax(scores, axis=-1)
        o = jnp.einsum('bhqk,bhkd->bhqd', p, v)
        o = o.transpose(0, 2, 1, 3).reshape(b, t, m)
        return o @ wo.T + bo

    def _L1_ffn_ref(x, CB, SCB, bias):
        import jax, jax.numpy as jnp
        import numpy as np
        B, S, K, N = (8, 1024, 128, 128)
        out = jnp.einsum('bsk,nk->bsn', x, CB)
        out = out * (SCB * (1.0 / 127.0)) + bias
        return out
    x = L0_attn_x
    x = _layernorm(x + _L0_attn_ref(x, L0_attn_q_w, L0_attn_q_b, L0_attn_k_w, L0_attn_k_b, L0_attn_v_w, L0_attn_v_b, L0_attn_l_w, L0_attn_l_b), axis=-1)
    x = _layernorm(x + _L0_ffn_ref(x, L0_ffn_gate_w, L0_ffn_gate_bias, L0_ffn_Wg, L0_ffn_Wu, L0_ffn_Wd, L0_ffn_Sg, L0_ffn_Su, L0_ffn_Sd), axis=-1)
    x = _layernorm(x + _L1_attn_ref(x, L1_attn_wq, L1_attn_bq, L1_attn_wk, L1_attn_bk, L1_attn_wv, L1_attn_bv, L1_attn_wo, L1_attn_bo, L1_attn_rot_cos, L1_attn_rot_sin), axis=-1)
    x = _layernorm(x + _L1_ffn_ref(x, L1_ffn_CB, L1_ffn_SCB, L1_ffn_bias), axis=-1)
    return x

_drawn_inputs = setup_inputs


def setup_inputs(seed=0):
    import zlib

    import numpy as np

    out = dict(_drawn_inputs(seed))
    spreads = {'L1_attn_bq': (0.0, 0.75),
     'L1_attn_bk': (0.0, 0.693),
     'L1_attn_bv': (0.0, 0.1),
     'L1_attn_bo': (0.0, 0.1)}
    factors = {'L0_attn_q_b': 8.0,
     'L0_attn_k_b': 8.0,
     'L0_ffn_gate_w': 8.0,
     'L0_ffn_gate_bias': 8.0,
     'L0_ffn_Wg': 8.0,
     'L0_ffn_Wu': 8.0,
     'L0_ffn_Wd': 8.0,
     'L0_ffn_Sg': 8.0,
     'L0_ffn_Su': 8.0,
     'L0_ffn_Sd': 8.0,
     'L1_ffn_bias': 8.0}
    for name, (base, spread) in spreads.items():
        noise = np.random.default_rng([zlib.crc32(name.encode()), seed]).standard_normal(out[name].shape)
        drawn = base * np.exp(spread * noise) if base else spread * noise
        out[name] = jnp.asarray(drawn.astype(out[name].dtype))
    for name, factor in factors.items():
        out[name] = (out[name] * factor).astype(out[name].dtype)
    return out
```

```python
import concourse.bass as bass
from concourse import mybir
from contextlib import ExitStack

FP32 = mybir.dt.float32
F32R = mybir.dt.float32r
ALU = mybir.AluOpType
ACT = mybir.ActivationFunctionType
AX = mybir.AxisListType

P = 128
NB, S, D = 16, 256, 128
TOK = NB * S
NT = TOK // P
TB = S // P
EPS = 1e-5

H0, P0 = 16, 64
NJ = H0 // 2

E, I = 64, 88
NG, GE = 8, 8
KEEP_GROUPS = 4
ROUTED_SCALE = 2.5
FF = E * I + 2 * I
NC = (FF + P - 1) // P
NCR = E * I // P
TILE = 512
NTILE = TOK // TILE
SUB = TILE // P
FAR = 3.0e38

H1, D1 = 16, 8
CH = D // D1
HT = S // H1
GRP = 4
W32 = 32


def build(nc, t):
    t_out = t["out"]
    with ExitStack() as ctx:
        def sb(name, shape, dt=FP32, stage=ctx):
            return stage.enter_context(nc.sbuf_tensor(name, shape, dt))

        def sem(name):
            return ctx.enter_context(nc.semaphore(name))

        bank = [ctx.enter_context(nc.psum_tensor(f"bank{i}", [P, 512], FP32)) for i in range(8)]

        x1_d = nc.dram_tensor("x1_d", [TOK, D], FP32, kind="Internal").ap()
        x1T_d = nc.dram_tensor("x1T_d", [D, TOK], FP32, kind="Internal").ap()
        rwT_d = nc.dram_tensor("rwT_d", [P, TOK], FP32, kind="Internal").ap()
        x2_d = nc.dram_tensor("x2_d", [TOK, D], FP32, kind="Internal").ap()
        x2T_d = nc.dram_tensor("x2T_d", [D, TOK], FP32, kind="Internal").ap()

        ident = sb("ident", [P, P])
        minus_half = sb("minus_half", [P, 4])
        eps = sb("eps", [P, 4])
        one = sb("one", [P, 1])
        waited = sb("waited", [P, 1])
        st6 = sb("st6", [P, SUB, 6])
        mv = sb("mv", [P, SUB, 2])
        veps = sb("veps", [P, SUB])
        rstd = sb("rstd", [P, SUB])

        st_w = ExitStack()
        ctx_sb = sb
        sb = lambda name, shape, dt=FP32: ctx_sb(name, shape, dt, st_w)
        w_hi = sb("w_hi", [P, NC, 3, P], F32R)
        w_raw = sb("w_raw", [P, 2, 3, P])
        select = sb("select", [P, NCR, P], F32R)
        xf = sb("xf", [P, TILE])
        rw_in = [sb(f"rw_in{i}", [P, TILE], F32R) for i in range(2)]
        xres = sb("xres", [P, SUB, D])

        st_a = ExitStack()
        sb = lambda name, shape, dt=FP32: ctx_sb(name, shape, dt, st_a)
        xT = sb("xT", [P, TOK])
        wq = sb("wq", [P, H0 * P0])
        wk = sb("wk", [P, H0 * P0])
        wv = sb("wv", [P, H0 * P0])
        lw = sb("lw", [P, NJ, D])
        qb = sb("qb", [P, NJ])
        qb8 = sb("qb8", [P, NJ])
        kb_ = sb("kb", [P, NJ])
        vb = sb("vb", [P, H0 * P0])
        lb = sb("lb", [P, D])
        gate_w = sb("gate_w", [P, E])
        gate_b = sb("gate_b", [P, E])
        tri = sb("tri", [P, NG, NG])
        xv = sb("xv", [P, S])
        xr = sb("xr", [P, TB, D])
        xrl = sb("xrl", [P, TB, D])
        v_sb = sb("v_sb", [P, TB, H0 * P0])
        q_sb = [sb(f"q_sb{i}", [P, 2, S]) for i in range(2)]
        k_sb = [sb(f"k_sb{i}", [P, S]) for i in range(2)]
        e_sb = [sb(f"e_sb{i}", [P, 2, TB, S]) for i in range(2)]
        vn_sb = [sb(f"vn_sb{i}", [P, TB, 2, P0]) for i in range(2)]
        nmax = sb("nmax", [P, NJ, TB, 2])
        esum = sb("esum", [P, NJ, TB, 2])
        erec = sb("erec", [P, NJ, TB, 2])
        ctxT = sb("ctxT", [P, NJ, S])
        y_sb = sb("y_sb", [P, TB, D])
        rwTs = sb("rwTs", [P, S], F32R)
        x1s = sb("x1s", [P, TB, D])
        x1Ts = sb("x1Ts", [P, S])
        r_exp = sb("r_exp", [P, TB, E])
        r_one = sb("r_one", [P, TB, E])
        score = sb("score", [P, TB, E])
        choice = sb("choice", [P, TB, E])
        top = sb("top", [P, TB, NG, 8])
        gsum = sb("gsum", [P, TB, NG])
        g_gt = sb("g_gt", [P, TB, NG, NG])
        g_eq = sb("g_eq", [P, TB, NG, NG])
        g_tie = sb("g_tie", [P, TB, NG, NG])
        g_cnt = sb("g_cnt", [P, TB, NG, NG])
        rank = sb("rank", [P, TB, NG])
        gmask = sb("gmask", [P, TB, NG])
        masked = sb("masked", [P, TB, E])
        masked0 = sb("masked0", [P, TB, E])
        top8 = sb("top8", [P, TB, 8])
        marked = sb("marked", [P, TB, E])
        sel = sb("sel", [P, TB, E])
        wsel = sb("wsel", [P, TB, E])
        wsum = sb("wsum", [P, TB])
        wsum2 = sb("wsum2", [P, TB])
        wrec = sb("wrec", [P, TB])
        wrec2 = sb("wrec2", [P, TB])
        rw = sb("rw", [P, TB, E])
        rw_hi = sb("rw_hi", [P, TB, E], F32R)
        rw_st = sb("rw_st", [P, TB, 2, E])
        st_a.close()
        sb = ctx_sb

        st_b = ExitStack()
        sb = lambda name, shape, dt=FP32: ctx_sb(name, shape, dt, st_b)
        w_lo = sb("w_lo", [P, NC, 3, P], F32R)
        x_hi = [sb(f"x_hi{i}", [P, TILE], F32R) for i in range(2)]
        x_lo = [sb(f"x_lo{i}", [P, TILE], F32R) for i in range(2)]
        sg = [sb(f"sg{i}", [P, TILE]) for i in range(2)]
        hf = [sb(f"hf{i}", [P, TILE]) for i in range(2)]
        h_hi = [sb(f"h_hi{i}", [P, TILE], F32R) for i in range(2)]
        h_lo = [sb(f"h_lo{i}", [P, TILE], F32R) for i in range(2)]
        oT = sb("oT", [P, TILE])
        y2 = sb("y2", [P, SUB, D])
        x2s = sb("x2s", [P, SUB, D])
        x2Ts = sb("x2Ts", [P, TILE])
        st_b.close()
        st_w.close()
        sb = ctx_sb

        st_c = ExitStack()
        sb = lambda name, shape, dt=FP32: ctx_sb(name, shape, dt, st_c)
        c_w = [sb(f"c_w{i}", [P, CH, W32]) for i in range(3)]
        c_ws = [sb(f"c_ws{i}", [P, CH, W32]) for i in range(2)]
        c_wt = [sb(f"c_wt{i}", [P, CH, W32]) for i in range(4)]
        c_wr = [sb(f"c_wr{i}", [P, CH, W32]) for i in range(2)]
        c_b = sb("c_b", [P, 3, CH])
        c_bs = sb("c_bs", [P, 2, CH])
        c_bt = sb("c_bt", [P, 4, CH])
        c_br = sb("c_br", [P, 3, CH])
        c_cos = sb("c_cos", [P, W32])
        c_sin = sb("c_sin", [P, W32])
        c_sgn = sb("c_sgn", [P, W32])
        c_sins = sb("c_sins", [P, W32])
        c_cosp = sb("c_cosp", [P, 1])
        c_sinp = sb("c_sinp", [P, 1])
        c_sgnp = sb("c_sgnp", [P, 1])
        c_sinsp = sb("c_sinsp", [P, 1])
        c_spec = sb("c_spec", [P, 3])
        c_low = sb("c_low", [P, 2])
        c_wo = sb("c_wo", [P, D])
        c_bo = sb("c_bo", [P, D])
        c_cb = sb("c_cb", [P, D])
        c_scb = sb("c_scb", [P, D])
        c_scale = sb("c_scale", [P, D])
        c_fb = sb("c_fb", [P, D])
        x_kv = sb("x_kv", [P, 2 * S])
        x_q = sb("x_q", [P, 2 * S])
        qk_st = sb("qk_st", [P, 2, 8, 2, CH, HT])
        v_st = sb("v_st", [P, 8, CH, HT])
        qk_hi = [sb(f"qk_hi{i}", [P, 2, S], F32R) for i in range(2)]
        q_m = [sb(f"q_m{i}", [P, 4, S], F32R) for i in range(2)]
        k_m = [sb(f"k_m{i}", [P, 4, S], F32R) for i in range(2)]
        k_alone = [sb(f"k_alone{i}", [P, 4, GRP, S], F32R) for i in range(2)]
        q_x = [sb(f"q_x{i}", [P, 4, S], F32R) for i in range(2)]
        mx = [sb(f"mx{i}", [P, TB, GRP]) for i in range(2)]
        mx_hi = sb("mx_hi", [P, TB, GRP], F32R)
        mx_pad = sb("mx_pad", [P, TB, GRP, W32])
        vt = [sb(f"vt{i}", [P, 4, TB, P]) for i in range(2)]
        pt = [sb(f"pt{i}", [P, GRP, TB, S]) for i in range(2)]
        aT = [sb(f"aT{i}", [P, 4, S]) for i in range(2)]
        den = sb("den", [P, TB, H1])
        an = sb("an", [P, TB, D])
        anT = sb("anT", [P, S])
        xr3 = sb("xr3", [P, TB, D])
        xr3b = sb("xr3b", [P, TB, D])
        y3 = sb("y3", [P, TB, D])
        x3s = sb("x3s", [P, TB, D])
        x3b = sb("x3b", [P, TB, D])
        x3T = sb("x3T", [P, S])
        z0 = sb("z0", [P, TB, D])
        z1 = sb("z1", [P, TB, D])
        res = sb("res", [P, TB, D])
        ln_st = [sb(f"ln_st{i}", [P, TB, 6]) for i in range(2)]
        ln_mv = [sb(f"ln_mv{i}", [P, TB, 2]) for i in range(2)]
        ln_ve = [sb(f"ln_ve{i}", [P, TB]) for i in range(2)]
        ln_rs = [sb(f"ln_rs{i}", [P, TB]) for i in range(2)]
        st_c.close()
        sb = ctx_sb

        ps_qk, ps_s, ps_c, ps_v, ps_o = bank[0], bank[1:5], bank[5], bank[6], bank[7]

        consts = sem("consts")
        const_ready = sem("const_ready")
        zeros_ready = sem("zeros_ready")
        x_all = sem("x_all")
        xv_loaded = sem("xv_loaded")
        xr_loaded = sem("xr_loaded")
        xrl_ready = sem("xrl_ready")
        qb8_ready = sem("qb8_ready")
        v_done = sem("v_done")
        v_ready = sem("v_ready")
        qk_done = sem("qk_done")
        qk_ready = sem("qk_ready")
        s_done = sem("s_done")
        max_ready = sem("max_ready")
        e_ready = sem("e_ready")
        rec_ready = sem("rec_ready")
        vn_ready = sem("vn_ready")
        c_done = sem("c_done")
        c_ready = sem("c_ready")
        o_done = sem("o_done")
        y_ready = sem("y_ready")
        stats_ready = sem("stats_ready")
        mv_ready = sem("mv_ready")
        veps_ready = sem("veps_ready")
        rstd_ready = sem("rstd_ready")
        x1_ready = sem("x1_ready")
        x1_stored = sem("x1_stored")
        x1T_done = sem("x1T_done")
        x1T_ready = sem("x1T_ready")
        x1T_stored = sem("x1T_stored")
        rwT_stored = sem("rwT_stored")
        logit_done = sem("logit_done")
        r_exp_ready = sem("r_exp_ready")
        rt = sem("rt")
        rw_ready = sem("rw_ready")
        rwT_done = sem("rwT_done")
        rwT_ready = sem("rwT_ready")
        block = ctx.enter_context(nc.Block())

        def own_wait():
            nc.vector.memset(waited[:, :], 0.0)


        def a_v_part(b, half, kb):
            n = 2 * half + kb
            pe = nc.tensor
            if not (isinstance(b, int) and b == 0 and n == 0):
                pe.wait_ge(v_ready, 4 * b + n)
            if not (isinstance(b, int) and b < 2):
                if n == 0:
                    pe.wait_ge(r_exp_ready, b - 1)
                if n == 2:
                    pe.wait_ge(rwT_ready, b - 2)
            if kb == 0 and half == 0:
                pe.wait_ge(xv_loaded, 16 * (b + 1))
            nc.tensor.matmul(ps_v[:, :], xv[:, kb * P:(kb + 1) * P], wv[:, half * 512:(half + 1) * 512],
                             start=True, stop=True).then_inc(v_done, 1)

        def a_qk(b, j):
            pe = nc.tensor
            g = 8 * b + j
            if not (isinstance(b, int) and b == 0 and j == 0):
                pe.wait_ge(qk_ready, 3 * g)
            xb = xT[:, bass.ds(b * S, S)]
            nc.tensor.matmul(ps_qk[:, 0:S], wq[:, j * P:(j + 1) * P], xb, start=True, stop=True)
            nc.tensor.matmul(ps_qk[:, S:2 * S], wk[:, j * P:(j + 1) * P], xb,
                             start=True, stop=True).then_inc(qk_done, 1)

        def a_scores(b, j):
            pe = nc.tensor
            g = 8 * b + j
            pe.wait_ge(qk_ready, 3 * (g + 1))
            if not (isinstance(b, int) and b == 0 and j < 2):
                pe.wait_ge(e_ready, 2 * (g - 1))
            for h in range(2):
                for kb in range(TB):
                    last = nc.tensor.matmul(ps_s[2 * (j % 2) + h][:, kb * S:(kb + 1) * S],
                                            k_sb[j % 2][:, kb * P:(kb + 1) * P], q_sb[j % 2][:, h, :],
                                            start=True, stop=True)
                last.then_inc(s_done, 1)

        def a_pv(b, j):
            pe = nc.tensor
            g = 8 * b + j
            pe.wait_ge(vn_ready, g + 1)
            pe.wait_ge(e_ready, 2 * (g + 1))
            if not (isinstance(b, int) and b == 0 and j < 1):
                pe.wait_ge(c_ready, g)
            for kb in range(TB):
                for h in range(2):
                    lo = h * P0
                    last = nc.tensor.matmul(ps_c[lo:lo + P0, (j % 2) * S:(j % 2 + 1) * S],
                                            vn_sb[j % 2][:, kb, h, :], e_sb[j % 2][:, h, kb, :],
                                            start=(kb == 0), stop=(kb == TB - 1))
            last.then_inc(c_done, 1)

        def a_out(b):
            pe = nc.tensor
            pe.wait_ge(c_ready, 8 * (b + 1))
            if not (isinstance(b, int) and b == 0):
                pe.wait_ge(x1T_ready, b)
            for tb in range(TB):
                for j in range(NJ):
                    last = nc.tensor.matmul(ps_o[:, tb * P:(tb + 1) * P], ctxT[:, j, tb * P:(tb + 1) * P],
                                            lw[:, j, :], start=(j == 0), stop=(j == NJ - 1))
            last.then_inc(o_done, 1)

        def a_x1T(b):
            nc.tensor.wait_ge(x1_ready, TB * (b + 1))
            nc.tensor.wait_ge(y_ready, b + 1)
            for tb in range(TB):
                last = nc.tensor.transpose(ps_o[:, tb * P:(tb + 1) * P], x1s[:, tb, :], ident[:, :])
            last.then_inc(x1T_done, 1)

        def a_logits(b, v_parts):
            nc.tensor.wait_ge(x1T_ready, b + 1)
            nc.tensor.wait_ge(v_ready, v_parts)
            for tb in range(TB):
                last = nc.tensor.matmul(ps_v[:, tb * E:(tb + 1) * E], x1Ts[:, tb * P:(tb + 1) * P],
                                        gate_w[:, :], start=True, stop=True)
            last.then_inc(logit_done, 1)

        def a_rwT(b, v_parts, logits):
            nc.tensor.wait_ge(rw_ready, 2 * (b + 1))
            nc.tensor.wait_ge(v_ready, v_parts)
            nc.tensor.wait_ge(r_exp_ready, logits)
            if not (isinstance(b, int) and b == 0):
                nc.tensor.wait_ge(rwT_ready, b)
            for tb in range(TB):
                last = nc.tensor.transpose(ps_v[:, tb * P:(tb + 1) * P],
                                           rw_st[:, tb].rearrange("p a e -> p (a e)"), ident[:, :])
            last.then_inc(rwT_done, 1)

        def pair(b, j):
            return (b - 1, j + NJ) if j < 0 else (b + 1, j - NJ) if j >= NJ else (b, j)

        def a_pe_batch(b, first, second, last):
            for j in range(NJ):
                if j < 6 or not last:
                    a_qk(*pair(b, j + 2))
                if j > 0 or not first:
                    a_pv(*pair(b, j - 1))
                if j < 7 or not last:
                    a_scores(*pair(b, j + 1))
                if j == 0 and not first:
                    a_out(b - 1)
                if j in (1, 2):
                    a_v_part(b, 1, j - 1)
                if j in (5, 6) and not last:
                    a_v_part(b + 1, 0, j - 5)
                if not first:
                    if j == 3:
                        a_x1T(b - 1)
                    if j == 4:
                        a_logits(b - 1, 4 * b + 4)
                if not second:
                    if j == 7:
                        a_rwT(b - 2, 4 * b + (4 if last else 6), b)

        def a_qk_out(b, j):
            g = 8 * b + j
            nc.scalar.wait_ge(qk_done, g + 1)
            for h in range(2):
                lo = h * P0
                nc.scalar.activation(q_sb[j % 2][lo:lo + P0, h, :], ps_qk[lo:lo + P0, 0:S], ACT.Identity,
                                     bias=qb8[lo:lo + P0, j:j + 1], scale=0.125).then_inc(qk_ready, 1)
            nc.scalar.activation(k_sb[j % 2][:, :], ps_qk[:, S:2 * S], ACT.Identity, bias=kb_[:, j:j + 1],
                                 scale=1.0).then_inc(qk_ready, 1)

        def a_exp(b, j):
            g = 8 * b + j
            for h in range(2):
                nc.scalar.wait_ge(max_ready, 2 * g + h + 1)
                for kb in range(TB):
                    last = nc.scalar.activation(e_sb[j % 2][:, h, kb, :],
                                                ps_s[2 * (j % 2) + h][:, kb * S:(kb + 1) * S], ACT.Exp,
                                                bias=nmax[:, j, kb, h:h + 1], scale=1.0,
                                                accum_out=esum[:, j, kb, h:h + 1])
                last.then_inc(e_ready, 1)

        def a_x1T_out(b):
            nc.scalar.wait_ge(x1T_done, b + 1)
            if not (isinstance(b, int) and b == 0):
                nc.scalar.wait_ge(x1T_stored, 16 * b)
            nc.scalar.copy(x1Ts[:, :], ps_o[:, 0:S]).then_inc(x1T_ready, 1)

        def a_r_exp(b):
            nc.scalar.wait_ge(logit_done, b + 1)
            nc.scalar.activation(r_exp[:, :, :].rearrange("p t e -> p (t e)"), ps_v[:, 0:TB * E], ACT.Exp,
                                 scale=-1.0).then_inc(r_exp_ready, 1)

        def a_rwT_out(b):
            nc.scalar.wait_ge(rwT_done, b + 1)
            if not (isinstance(b, int) and b == 0):
                nc.scalar.wait_ge(rwT_stored, 16 * b)
            nc.scalar.copy(rwTs[:, :], ps_v[:, 0:S]).then_inc(rwT_ready, 1)

        def a_act_batch(b, first, second, last):
            for j in range(NJ):
                if j < 6 or not last:
                    a_qk_out(*pair(b, j + 2))
                if j == 5 and not first:
                    a_r_exp(b - 1)
                if j < 7 or not last:
                    a_exp(*pair(b, j + 1))
                if j == 3 and not first:
                    a_x1T_out(b - 1)
                if not second:
                    if j == 7:
                        a_rwT_out(b - 2)

        def a_max(b, j):
            for h in range(2):
                nc.vector.wait_ge(s_done, 2 * (8 * b + j) + h + 1)
                nc.vector.tensor_reduce(nmax[:, j, :, h],
                                        ps_s[2 * (j % 2) + h][:, :].rearrange("p (k q) -> p k q", k=TB),
                                        AX.X, ALU.max, negate=True).then_inc(max_ready, 1)

        def a_rec(b, j):
            nc.vector.wait_ge(e_ready, 2 * (8 * b + j + 1))
            nc.vector.reciprocal(erec[:, j], esum[:, j]).then_inc(rec_ready, 1)

        def a_c_out(b, j):
            nc.vector.wait_ge(c_done, 8 * b + j + 1)
            nc.vector.tensor_copy(ctxT[:, j, :], ps_c[:, (j % 2) * S:(j % 2 + 1) * S]).then_inc(c_ready, 1)

        def a_v_out(b, half, kb):
            nc.vector.wait_ge(v_done, 4 * b + 2 * half + kb + 1)
            if not (isinstance(b, int) and b == 0):
                nc.vector.wait_ge(vn_ready, 8 * b if half else 8 * b - 4)
            cols = slice(half * 512, (half + 1) * 512)
            nc.vector.tensor_tensor(v_sb[:, kb, cols], ps_v[:, :], vb[:, cols], ALU.add).then_inc(v_ready, 1)

        def a_y(b):
            nc.vector.wait_ge(o_done, b + 1)
            nc.vector.wait_ge(xrl_ready, b + 1)
            nc.vector.tensor_tensor(y_sb[:, 0:TB, :], ps_o[:, 0:S].rearrange("p (t d) -> p t d", t=TB),
                                    xrl[:, :, :], ALU.add).then_inc(y_ready, 1)
            nc.vector.wait_ge(y_ready, b + 1)
            for tb in range(TB):
                nc.vector.bn_stats(st6[:, tb, :], y_sb[:, tb, :]).then_inc(stats_ready, 1)
            nc.vector.wait_ge(stats_ready, TB * (b + 1))
            own_wait()
            for tb in range(TB):
                nc.vector.bn_aggr(mv[:, tb, :], st6[:, tb, :]).then_inc(mv_ready, 1)

        def a_norm(b):
            nc.vector.wait_ge(rstd_ready, b + 1)
            if not (isinstance(b, int) and b == 0):
                nc.vector.wait_ge(x1_stored, 16 * b)
            for tb in range(TB):
                nc.vector.tensor_scalar(x1s[:, tb, :], y_sb[:, tb, :], mv[:, tb, 0:1], rstd[:, tb:tb + 1],
                                        ALU.subtract, ALU.mult).then_inc(x1_ready, 1)

        ROUTE_STEPS = 20

        def router(b, n):
            n = [n]

            def step(ins):
                n[0] += 1
                ins.then_inc(rt, 1)
                nc.vector.wait_ge(rt, ROUTE_STEPS * b + n[0])

            return step

        def route_scores(b):
            step = router(b, 0)
            v = nc.vector
            v.wait_ge(r_exp_ready, b + 1)
            step(v.tensor_scalar(r_one[:], r_exp[:], 1.0, None, ALU.add))
            step(v.reciprocal(score[:], r_one[:]))
            step(v.tensor_tensor(choice[:], score[:], gate_b[:, :].unsqueeze(1).broadcast_to([P, TB, E]), ALU.add))

        def route_best_two(b):
            step = router(b, 3)
            v = nc.vector
            for tb in range(TB):
                for g in range(NG):
                    last = v.max(top[:, tb, g, :], choice[:, tb, g * GE:(g + 1) * GE])
            step(last)
            step(v.tensor_tensor(gsum[:], top[:, :, :, 0], top[:, :, :, 1], ALU.add))

        def route_groups(b):
            step = router(b, 5)
            v = nc.vector
            mine = gsum[:].unsqueeze(3).broadcast_to([P, TB, NG, NG])
            other = gsum[:].unsqueeze(2).broadcast_to([P, TB, NG, NG])
            v.tensor_tensor(g_gt[:], other, mine, ALU.is_gt)
            step(v.tensor_tensor(g_eq[:], other, mine, ALU.is_equal))
            step(v.tensor_tensor(g_tie[:], g_eq[:], tri[:].unsqueeze(1).broadcast_to([P, TB, NG, NG]), ALU.mult))
            step(v.tensor_tensor(g_cnt[:], g_gt[:], g_tie[:], ALU.add))
            step(v.tensor_reduce(rank[:], g_cnt[:], AX.X, ALU.add))
            step(v.tensor_scalar(gmask[:], rank[:], float(KEEP_GROUPS), None, ALU.is_lt))

        def route_best_eight(b):
            step = router(b, 10)
            v = nc.vector
            grouped = lambda a: a[:].rearrange("p t (g e) -> p (t g) e", g=NG)
            step(v.tensor_tensor(grouped(masked), grouped(choice),
                                 gmask[:].rearrange("p t g -> p (t g)").unsqueeze(2).broadcast_to([P, TB * NG, GE]),
                                 ALU.mult))
            step(v.tensor_scalar(masked0[:], masked[:], 0.0, None, ALU.add))
            own_wait()
            for tb in range(TB):
                last = v.max(top8[:, tb, :], masked0[:, tb, :])
            step(last)
            own_wait()
            for tb in range(TB):
                last = v.match_replace(marked[:, tb, :], top8[:, tb, :], masked0[:, tb, :], FAR)
            step(last)
            step(v.tensor_scalar(sel[:], marked[:], 0.5 * FAR, None, ALU.is_ge))

        def route_weights(b):
            step = router(b, 15)
            v = nc.vector
            step(v.tensor_tensor(wsel[:], score[:], sel[:], ALU.mult))
            step(v.tensor_reduce(wsum[:], wsel[:], AX.X, ALU.add))
            step(v.tensor_scalar(wsum2[:], wsum[:], 1e-20, None, ALU.add))
            step(v.reciprocal(wrec[:], wsum2[:]))
            step(v.tensor_scalar(wrec2[:], wrec[:], ROUTED_SCALE, None, ALU.mult))
            if not (isinstance(b, int) and b == 0):
                v.wait_ge(rwT_done, b)
            for tb in range(TB):
                last = v.tensor_scalar(rw[:, tb, :], wsel[:, tb, :], wrec2[:, tb:tb + 1], None, ALU.mult)
            last.then_inc(rw_full, 1)
            v.wait_ge(rw_full, b + 1)
            v.tensor_copy(rw_hi[:], rw[:]).then_inc(rw_split, 1)
            v.wait_ge(rw_split, b + 1)
            v.tensor_copy(rw_st[:, :, 0, :], rw_hi[:].bitcast(FP32)).then_inc(rw_ready, 1)
            v.tensor_tensor(rw_st[:, :, 1, :], rw[:], rw_hi[:].bitcast(FP32), ALU.subtract).then_inc(rw_ready, 1)

        rw_full = sem("rw_full")
        rw_split = sem("rw_split")

        def a_dve_batch(b, first, second, last):
            for j in range(NJ):
                if j > 0 or not first:
                    a_c_out(*pair(b, j - 1))
                a_rec(b, j)
                if j < 7 or not last:
                    a_max(*pair(b, j + 1))
                if j in (1, 2):
                    a_v_out(b, 1, j - 1)
                if j in (5, 6) and not last:
                    a_v_out(b + 1, 0, j - 5)
                if not first:
                    if j == 1:
                        a_y(b - 1)
                    if j == 2:
                        a_norm(b - 1)
                    if j == 6:
                        route_scores(b - 1)
                    if j == 7:
                        route_best_two(b - 1)
                if not second:
                    if j == 0:
                        route_groups(b - 2)
                    if j == 3:
                        route_best_eight(b - 2)
                    if j == 4:
                        route_weights(b - 2)

        def a_vn(b, j):
            g = 8 * b + j
            p = nc.gpsimd
            p.wait_ge(v_ready, 4 * b + (2 if j < 4 else 4))
            p.wait_ge(rec_ready, g + 1)
            if not (isinstance(b, int) and b == 0 and j < 2):
                p.wait_ge(c_done, g - 1)
            p.tensor_tensor(vn_sb[j % 2][:], v_sb[:, :, j * P:(j + 1) * P].rearrange("p k (h d) -> p k h d", h=2),
                            erec[:, j].unsqueeze(3).broadcast_to([P, TB, 2, P0]), ALU.mult).then_inc(vn_ready, 1)

        def a_xrl(b):
            p = nc.gpsimd
            p.wait_ge(xr_loaded, 16 * (b + 1))
            if not (isinstance(b, int) and b == 0):
                p.wait_ge(y_ready, b)
            p.tensor_tensor(xrl[:], xr[:], lb[:].unsqueeze(1).broadcast_to([P, TB, D]), ALU.add).then_inc(xrl_ready, 1)

        def a_rstd(b):
            p = nc.gpsimd
            p.wait_ge(mv_ready, TB * (b + 1))
            p.tensor_tensor(veps[:, 0:TB], mv[:, 0:TB, 1], eps[:, 0:TB], ALU.add).then_inc(veps_ready, 1)
            p.wait_ge(veps_ready, b + 1)
            p.tensor_tensor(rstd[:, 0:TB], veps[:, 0:TB], minus_half[:, 0:TB], ALU.pow).then_inc(rstd_ready, 1)

        def a_pool_batch(b, first, second, last):
            for j in range(NJ):
                a_vn(b, j)
                if not first:
                    if j == 1:
                        a_rstd(b - 1)
                if j == 4:
                    a_xrl(b)

        def a_store_x1(b):
            nc.sync.wait_ge(x1_ready, TB * (b + 1))
            nc.sync.dma_start(x1_d.rearrange("(n p) d -> p n d", p=P)[:, bass.ds(b * TB, TB), :],
                              x1s[:]).then_inc(x1_stored, 16)
            nc.sync.wait_ge(x1T_ready, b + 1)
            nc.sync.dma_start(x1T_d[:, bass.ds(b * S, S)], x1Ts[:]).then_inc(x1T_stored, 16)

        def a_store_rwT(b):
            nc.sync.wait_ge(rwT_ready, b + 1)
            nc.sync.dma_start(rwT_d[:, bass.ds(b * S, S)], rwTs[:].bitcast(FP32)).then_inc(rwT_stored, 16)

        def a_sp_batch(b, first, second, last):
            if not last:
                nc.sync.wait_ge(v_done, 4 * (b + 1))
                nc.sync.dma_start(xv[:, :], t["xT"][:, bass.ds((b + 1) * S, S)]).then_inc(xv_loaded, 16)
            if not first:
                a_store_x1(b - 1)
            if not last:
                nc.sync.wait_ge(xrl_ready, b + 1)
                nc.sync.dma_start(xr[:], t["x"].rearrange("(n p) d -> p n d", p=P)[:, bass.ds((b + 1) * TB, TB), :]
                                  ).then_inc(xr_loaded, 16)
            if not second:
                a_store_rwT(b - 2)

        ps_g, ps_u, ps_r, ps_acc, ps_t = bank[0:2], bank[2:4], bank[4:6], bank[6], bank[7]

        w_hi_loaded = sem("w_hi_loaded")
        raw_loaded = [sem(f"raw_loaded{i}") for i in range(2)]
        lo_ready = sem("lo_ready")
        xf_loaded = sem("xf_loaded")
        rw_loaded = [sem(f"rw_loaded{i}") for i in range(2)]
        xres_loaded = sem("xres_loaded")
        x_hi_ready = sem("x_hi_ready")
        x_lo_ready = sem("x_lo_ready")
        g_done = sem("g_done")
        u_done = sem("u_done")
        r_done = sem("r_done")
        d_done = sem("d_done")
        sg_ready = sem("sg_ready")
        t_ready = sem("t_ready")
        hf_ready = sem("hf_ready")
        h_hi_ready = sem("h_hi_ready")
        h_lo_ready = sem("h_lo_ready")
        oT_ready = sem("oT_ready")
        ot_done = sem("ot_done")
        y2_ready = sem("y2_ready")
        stats2_ready = sem("stats2_ready")
        mv2_ready = sem("mv2_ready")
        veps2_ready = sem("veps2_ready")
        rstd2_ready = sem("rstd2_ready")
        x2_ready = sem("x2_ready")
        x2T_done = sem("x2T_done")
        x2T_ready = sem("x2T_ready")
        x2_stored = sem("x2_stored")
        x2T_stored = sem("x2T_stored")
        GATE, UP, DOWN = range(3)

        def past(n, c, lag):
            return not (isinstance(n, int) and n * NC + c < lag)

        def three(out, c, which, hi, lo, start, stop):
            nc.tensor.matmul(out, w_lo[:, c, which, :], hi, start=start, stop=False)
            nc.tensor.matmul(out, w_hi[:, c, which, :], lo, start=False, stop=False)
            return nc.tensor.matmul(out, w_hi[:, c, which, :], hi, start=False, stop=stop)

        def b_up(n, c, par):
            pe = nc.tensor
            s = n * NC + c
            q = n * NCR + c
            if c == 0:
                pe.wait_ge(x_hi_ready, n + 1)
                pe.wait_ge(x_lo_ready, n + 1)
            if isinstance(n, int) and n == 0:
                pe.wait_ge(lo_ready, c + 1)
            if past(n, c, 2):
                pe.wait_ge(sg_ready, s - 1)
            three(ps_g[c % 2][:, :], c, GATE, x_hi[par][:, :], x_lo[par][:, :], True, True).then_inc(g_done, 1)
            if past(n, c, 2):
                pe.wait_ge(t_ready, s - 1)
            three(ps_u[c % 2][:, :], c, UP, x_hi[par][:, :], x_lo[par][:, :], True, True).then_inc(u_done, 1)
            if c < NCR:
                if c == 0:
                    pe.wait_ge(rw_loaded[par], 8 * (n + 2 - par))
                if past(n, c, 2):
                    pe.wait_ge(hf_ready, q - 1)
                nc.tensor.matmul(ps_r[c % 2][:, :], select[:, c, :], rw_in[par][:, :],
                                 start=True, stop=True).then_inc(r_done, 1)

        def b_down(n, c):
            pe = nc.tensor
            s = n * NC + c
            pe.wait_ge(h_hi_ready, s + 1)
            pe.wait_ge(h_lo_ready, s + 1)
            if c == 0 and past(n, c, 1):
                pe.wait_ge(oT_ready, n)
            three(ps_acc[:, :], c, DOWN, h_hi[c % 2][:, :], h_lo[c % 2][:, :], c == 0,
                  c == NC - 1).then_inc(d_done, 1)

        def b_oT(n):
            nc.tensor.wait_ge(oT_ready, n + 1)
            if past(n, 0, 1):
                nc.tensor.wait_ge(x2T_ready, n)
            for k in range(SUB):
                last = nc.tensor.transpose(ps_t[:, k * P:(k + 1) * P], oT[:, k * P:(k + 1) * P], ident[:, :])
            last.then_inc(ot_done, 1)

        def b_x2T(n):
            nc.tensor.wait_ge(x2_ready, SUB * (n + 1))
            nc.tensor.wait_ge(y2_ready, n + 1)
            for k in range(SUB):
                last = nc.tensor.transpose(ps_t[:, k * P:(k + 1) * P], x2s[:, k, :], ident[:, :])
            last.then_inc(x2T_done, 1)

        def b_pe_tile(n, par, first):
            for c in range(NC):
                b_up(n, c, par)
                if c >= 2:
                    b_down(n, c - 2)
                elif not first:
                    b_down(n - 1, NC + c - 2)
                if not first:
                    if c == 2:
                        b_oT(n - 1)
                    if c == 12:
                        b_x2T(n - 1)

        def b_silu(n, c):
            s = n * NC + c
            nc.scalar.wait_ge(g_done, s + 1)
            if past(n, c, 2):
                nc.scalar.wait_ge(t_ready, s - 1)
            nc.scalar.activation(sg[c % 2][:, :], ps_g[c % 2][:, :], ACT.Silu).then_inc(sg_ready, 1)

        def b_h_hi(n, c):
            s = n * NC + c
            if c < NCR:
                nc.scalar.wait_ge(hf_ready, n * NCR + c + 1)
            else:
                nc.scalar.wait_ge(t_ready, s + 1)
            if past(n, c, 2):
                nc.scalar.wait_ge(d_done, s - 1)
            nc.scalar.copy(h_hi[c % 2][:, :], hf[c % 2][:, :]).then_inc(h_hi_ready, 1)

        def b_oT_out(n):
            nc.scalar.wait_ge(d_done, NC * (n + 1))
            if past(n, 0, 1):
                nc.scalar.wait_ge(ot_done, n)
            nc.scalar.copy(oT[:, :], ps_acc[:, :]).then_inc(oT_ready, 1)

        def b_x2T_out(n):
            nc.scalar.wait_ge(x2T_done, n + 1)
            if past(n, 0, 1):
                nc.scalar.wait_ge(x2T_stored, 16 * n)
            nc.scalar.copy(x2Ts[:, :], ps_t[:, :]).then_inc(x2T_ready, 1)

        def b_x_hi(n, par):
            nc.scalar.wait_ge(xf_loaded, 16 * (n + 1))
            nc.scalar.copy(x_hi[par][:, :], xf[:, :]).then_inc(x_hi_ready, 1)

        def b_act_tile(n, par, first, last):
            for c in range(NC):
                b_silu(n, c)
                if c >= 1:
                    b_h_hi(n, c - 1)
                elif not first:
                    b_h_hi(n - 1, NC - 1)
                if not first:
                    if c == 2:
                        b_oT_out(n - 1)
                    if c == 12:
                        b_x2T_out(n - 1)
                if c == 20 and not last:
                    b_x_hi(n + 1, 1 - par)

        def b_lo(c):
            nc.vector.wait_ge(raw_loaded[c % 2], 16 * (c // 2 + 1))
            nc.vector.tensor_tensor(w_lo[:, c], w_raw[:, c % 2], w_hi[:, c].bitcast(FP32),
                                    ALU.subtract).then_inc(lo_ready, 1)

        def b_h(n, c):
            v = nc.vector
            s = n * NC + c
            v.wait_ge(sg_ready, s + 1)
            v.wait_ge(u_done, s + 1)
            if past(n, c, 2):
                v.wait_ge(h_lo_ready, s - 1)
            v.tensor_tensor(hf[c % 2][:, :], sg[c % 2][:, :], ps_u[c % 2][:, :], ALU.mult).then_inc(t_ready, 1)
            if c < NCR:
                v.wait_ge(t_ready, s + 1)
                v.wait_ge(r_done, n * NCR + c + 1)
                v.tensor_tensor(hf[c % 2][:, :], hf[c % 2][:, :], ps_r[c % 2][:, :],
                                ALU.mult).then_inc(hf_ready, 1)

        def b_y(n):
            v = nc.vector
            v.wait_ge(ot_done, n + 1)
            v.wait_ge(xres_loaded, 16 * (n + 1))
            v.tensor_tensor(y2[:], ps_t[:, :].rearrange("p (k d) -> p k d", k=SUB), xres[:],
                            ALU.add).then_inc(y2_ready, 1)

        def b_stats(n):
            v = nc.vector
            v.wait_ge(y2_ready, n + 1)
            for k in range(SUB):
                v.bn_stats(st6[:, k, :], y2[:, k, :]).then_inc(stats2_ready, 1)

        def b_mv(n):
            v = nc.vector
            v.wait_ge(stats2_ready, SUB * (n + 1))
            own_wait()
            for k in range(SUB):
                v.bn_aggr(mv[:, k, :], st6[:, k, :]).then_inc(mv2_ready, 1)

        def b_norm(n, ks):
            v = nc.vector
            v.wait_ge(rstd2_ready, n + 1)
            if past(n, 0, 1):
                v.wait_ge(x2_stored, 16 * n)
            for k in ks:
                v.tensor_scalar(x2s[:, k, :], y2[:, k, :], mv[:, k, 0:1], rstd[:, k:k + 1],
                                ALU.subtract, ALU.mult).then_inc(x2_ready, 1)

        def b_dve_tile(n, first):
            for c in range(NC):
                if first and c + 2 < NC:
                    b_lo(c + 2)
                b_h(n, c)
                if not first:
                    if c == 3:
                        b_y(n - 1)
                    if c == 5:
                        b_stats(n - 1)
                    if c == 6:
                        b_mv(n - 1)
                    if c == 8:
                        b_norm(n - 1, (0, 1))
                    if c == 9:
                        b_norm(n - 1, (2, 3))

        def b_h_lo(n, c):
            p = nc.gpsimd
            s = n * NC + c
            p.wait_ge(h_hi_ready, s + 1)
            if past(n, c, 2):
                p.wait_ge(d_done, s - 1)
            p.tensor_tensor(h_lo[c % 2][:, :], hf[c % 2][:, :], h_hi[c % 2][:, :].bitcast(FP32),
                            ALU.subtract).then_inc(h_lo_ready, 1)

        def b_x_lo(n, par):
            p = nc.gpsimd
            p.wait_ge(x_hi_ready, n + 1)
            p.tensor_tensor(x_lo[par][:, :], xf[:, :], x_hi[par][:, :].bitcast(FP32),
                            ALU.subtract).then_inc(x_lo_ready, 1)

        def b_rstd(n):
            p = nc.gpsimd
            p.wait_ge(mv2_ready, SUB * (n + 1))
            p.tensor_tensor(veps[:, :], mv[:, :, 1], eps[:, :], ALU.add).then_inc(veps2_ready, 1)
            p.wait_ge(veps2_ready, n + 1)
            p.tensor_tensor(rstd[:, :], veps[:, :], minus_half[:, :], ALU.pow).then_inc(rstd2_ready, 1)

        def b_pool_tile(n, par, first, last):
            for c in range(NC):
                b_h_lo(n, c)
                if c == 6 and not first:
                    b_rstd(n - 1)
                if c == 21 and not last:
                    b_x_lo(n + 1, 1 - par)

        def b_load(n, par):
            sp = nc.sync
            if past(n, 0, 1):
                sp.wait_ge(x_lo_ready, n)
            sp.dma_start(xf[:, :], x1T_d[:, bass.ds(n * TILE, TILE)]).then_inc(xf_loaded, 16)
            if not (isinstance(n, int) and n < 2):
                sp.wait_ge(r_done, NCR * (n - 1))
            sp.dma_start(rw_in[par][:, :].bitcast(FP32), rwT_d[:, bass.ds(n * TILE, TILE)]).then_inc(rw_loaded[par], 16)

        def b_load_res(n):
            sp = nc.sync
            if past(n, 0, 1):
                sp.wait_ge(y2_ready, n)
            sp.dma_start(xres[:], x1_d.rearrange("(n p) d -> p n d", p=P)[:, bass.ds(n * SUB, SUB), :]
                         ).then_inc(xres_loaded, 16)

        def b_store(n):
            sp = nc.sync
            sp.wait_ge(x2_ready, SUB * (n + 1))
            sp.dma_start(x2_d.rearrange("(n p) d -> p n d", p=P)[:, bass.ds(n * SUB, SUB), :],
                         x2s[:]).then_inc(x2_stored, 16)
            sp.wait_ge(x2T_ready, n + 1)
            sp.dma_start(x2T_d[:, bass.ds(n * TILE, TILE)], x2Ts[:, :]).then_inc(x2T_stored, 16)

        def b_raw(c):
            if c >= 2:
                nc.sync.wait_ge(lo_ready, c - 1)
            nc.sync.dma_start(w_raw[:, c % 2], t["w_all"][:, c * 3 * P:(c + 1) * 3 * P]
                              .rearrange("p (a m) -> p a m", a=3)).then_inc(raw_loaded[c % 2], 16)

        def b_sp():
            sp = nc.sync
            sp.wait_ge(x1T_stored, 16 * NB)
            sp.wait_ge(x1_stored, 16 * NB)
            sp.wait_ge(rwT_stored, 16 * NB)
            b_load(0, 0)
            for c in range(NC):
                b_raw(c)
                if c == 8:
                    b_load(1, 1)
                    b_load_res(0)
            with sp.Fori(0, NTILE // 2 - 1) as k:
                n = k * 2 + 1
                b_load(n + 1, 0)
                b_load_res(n)
                b_store(n - 1)
                b_load(n + 2, 1)
                b_load_res(n + 1)
                b_store(n)
            b_load_res(NTILE - 1)
            b_store(NTILE - 2)
            b_store(NTILE - 1)
            sp.wait_ge(x2_stored, 16 * NTILE)
            sp.wait_ge(x2T_stored, 16 * NTILE)

        ps_m, ps_x, ps_pv, ps_p, ps_tr, ps_tail = bank[0:2], bank[2:4], bank[4], bank[5], bank[6], bank[7]
        NPAIR = NB // 2

        c_loaded = sem("c_loaded")
        c_prep = sem("c_prep")
        pad_ready = sem("pad_ready")
        x_kv_loaded = sem("x_kv_loaded")
        x_q_loaded = sem("x_q_loaded")
        p_done = sem("p_done")
        p_ready = sem("p_ready")
        hi_ready = sem("hi_ready")
        split_ready = sem("split_ready")
        alone_zeroed = sem("alone_zeroed")
        k_alone_ready = [sem(f"k_alone_ready{j}") for j in range(4)]
        m_done = sem("m_done")
        mx_ready = sem("mx_ready")
        mx_hi_ready = sem("mx_hi_ready")
        pad_set = sem("pad_set")
        t_done = sem("t_done")
        q_x_ready = sem("q_x_ready")
        x_done = sem("x_done")
        p_exp_ready = sem("p_exp_ready")
        pv_done = sem("pv_done")
        aT_ready = sem("aT_ready")
        atr_done = sem("atr_done")
        den_ready = sem("den_ready")
        an_ready = sem("an_ready")
        anT_done = sem("anT_done")
        anT_ready = sem("anT_ready")
        wo_done = sem("wo_done")
        xr3_loaded = sem("xr3_loaded")
        xr3b_ready = sem("xr3b_ready")
        y3_ready = sem("y3_ready")
        x3_ready = sem("x3_ready")
        x3b_ready = sem("x3b_ready")
        x3T_done = sem("x3T_done")
        x3T_ready = sem("x3T_ready")
        cb_done = sem("cb_done")
        z0_ready = sem("z0_ready")
        z1_ready = sem("z1_ready")
        res_ready = sem("res_ready")
        ln_st_ready = [sem(f"ln_st_ready{i}") for i in range(2)]
        ln_mv_ready = [sem(f"ln_mv_ready{i}") for i in range(2)]
        ln_ve_ready = [sem(f"ln_ve_ready{i}") for i in range(2)]
        ln_rs_ready = [sem(f"ln_rs_ready{i}") for i in range(2)]
        out_stored = sem("out_stored")

        def whole(b):
            return isinstance(b, int)

        USES = [{(0, 0): ("vt", 0, 0), (0, 1): ("vt", 1, 0), (0, 2): ("k", 0, 1), (0, 3): ("k", 1, 1),
                 (1, 0): ("vt", 2, 0), (1, 1): ("vt", 3, 0), (1, 3): ("k", 2, 1), (2, 0): ("k", 3, 1),
                 (2, 2): ("v", 0, 1), (3, 0): ("v", 1, 1)},
                {(0, 1): ("q", 0, 2), (0, 3): ("v", 2, 1), (1, 1): ("v", 3, 1), (1, 3): ("q", 1, 2),
                 (2, 1): ("q", 2, 2), (3, 0): ("q", 3, 2)}]
        START = [("q", i, 1) for i in range(4)] + [("k", i, 1) for i in range(4)] + [("v", i, 1) for i in range(2)]

        def wanted(p, what, ahead):
            return not whole(p) or 0 <= p + ahead < NPAIR

        def use(p, u, k):
            if not whole(p):
                return 16 * (p + 1) + 10 * u + k
            n = 0
            for pp in range(-1, p + 1):
                for uu in range(2):
                    uses = START if (pp, uu) == (-1, 0) else list(USES[uu].values())
                    if (pp, uu) == (p, u):
                        return n + sum(wanted(pp, w, a) for w, _, a in uses[:k])
                    n += sum(wanted(pp, w, a) for w, _, a in uses)

        def c_project(p, what, part, n, ahead):
            pe = nc.tensor
            pe.wait_ge(p_ready, n)
            src = x_q if what == "q" else x_kv
            if what == "q":
                pe.wait_ge(x_q_loaded, 16 * (p + ahead + 1))
            else:
                pe.wait_ge(x_kv_loaded, 16 * (p + ahead + 1))
            w = c_w[2] if what == "v" else c_wr["qk".index(what)]
            xs = src[:, :].rearrange("p (a g i) -> p a g i", a=8, g=GRP)
            for i in range(4):
                for g in range(GRP):
                    last = nc.tensor.matmul(ps_p[W32 * g:W32 * (g + 1), i * P:(i + 1) * P], w[:, 4 * part + i, :],
                                            xs[:, :, g, :], start=True, stop=True, skip_group_check=True)
            last.then_inc(p_done, 1)

        def c_vt(p, part, n):
            nc.tensor.wait_ge(p_ready, n)
            for k in range(4):
                src = v_st[:, 2 * part + k // 2].rearrange("p c i -> p (c i)")
                last = nc.tensor.transpose(ps_p[:, k * P:(k + 1) * P], src[:, (k % 2) * P:(k % 2 + 1) * P],
                                           ident[:, :])
            last.then_inc(p_done, 1)

        def c_m(b, u, j, g):
            pe = nc.tensor
            n = 16 * b + 4 * j + g
            if g == 0:
                pe.wait_ge(split_ready, 2 * (4 * b + j + 1))
                pe.wait_ge(k_alone_ready[j], 16 * GRP * (b + 1))
            if not (whole(b) and n < 2):
                pe.wait_ge(mx_ready, n - 1)
            for qb in range(TB):
                last = nc.tensor.matmul(ps_m[g % 2][:, qb * S:(qb + 1) * S],
                                        q_m[u][:, j, qb * P:(qb + 1) * P], k_alone[u][:, j, g, :],
                                        start=True, stop=True)
            last.then_inc(m_done, 1)

        def c_t(b, j):
            pe = nc.tensor
            pe.wait_ge(pad_set, 2 * (4 * b + j + 1))
            if not (whole(b) and 4 * b + j == 0):
                pe.wait_ge(q_x_ready, 4 * b + j)
            for qb in range(TB):
                last = nc.tensor.transpose(ps_tr[:, qb * P:(qb + 1) * P],
                                           mx_pad[:, qb].rearrange("p g w -> p (g w)"), ident[:, :])
            last.then_inc(t_done, 1)

        def c_x(b, u, j, g):
            pe = nc.tensor
            n = 16 * b + 4 * j + g
            if g == 0:
                pe.wait_ge(q_x_ready, 4 * b + j + 1)
            if not (whole(b) and n < 2):
                pe.wait_ge(p_exp_ready, n - 1)
            for kb in range(TB):
                last = nc.tensor.matmul(ps_x[g % 2][:, kb * S:(kb + 1) * S],
                                        k_alone[u][:, j, g, kb * P:(kb + 1) * P], q_x[u][:, j, :],
                                        start=True, stop=True)
            last.then_inc(x_done, 1)

        def c_pv(b, u, p, j):
            pe = nc.tensor
            pe.wait_ge(p_exp_ready, 16 * b + 4 * j + 4)
            pe.wait_ge(p_ready, use(p, 0, (2 if j >= 2 else 1) if u == 0 else 6))
            if not (whole(b) and 4 * b + j == 0):
                pe.wait_ge(aT_ready, 4 * b + j)
            for kb in range(TB):
                for g in range(GRP):
                    lo = W32 * g
                    last = nc.tensor.matmul(ps_pv[lo:lo + W32, 0:S], vt[u][:, j, kb, lo:lo + W32],
                                            pt[j % 2][:, g, kb, :], start=(kb == 0), stop=(kb == TB - 1))
            last.then_inc(pv_done, 1)

        def c_atr(t, u, tb):
            pe = nc.tensor
            if tb == 0:
                pe.wait_ge(aT_ready, 4 * t + 4)
                if not (whole(t) and t == 0):
                    pe.wait_ge(z0_ready, t)
            else:
                pe.wait_ge(an_ready, 2 * t + 1)
            for j in range(4):
                last = nc.tensor.transpose(ps_tail[:, j * P:(j + 1) * P], aT[u][:, j, tb * P:(tb + 1) * P],
                                           ident[:, :])
            last.then_inc(atr_done, 1)

        def c_anT(t):
            nc.tensor.wait_ge(an_ready, 2 * t + 2)
            for tb in range(TB):
                last = nc.tensor.transpose(ps_tail[:, tb * P:(tb + 1) * P], an[:, tb, :], ident[:, :])
            last.then_inc(anT_done, 1)

        def c_wo_mm(t):
            nc.tensor.wait_ge(anT_ready, t + 1)
            for tb in range(TB):
                last = nc.tensor.matmul(ps_tail[:, tb * P:(tb + 1) * P], anT[:, tb * P:(tb + 1) * P], c_wo[:, :],
                                        start=True, stop=True)
            last.then_inc(wo_done, 1)

        def c_x3T(t):
            nc.tensor.wait_ge(x3_ready, 2 * t + 2)
            for tb in range(TB):
                last = nc.tensor.transpose(ps_tail[:, tb * P:(tb + 1) * P], x3s[:, tb, :], ident[:, :])
            last.then_inc(x3T_done, 1)

        def c_linear(t):
            nc.tensor.wait_ge(x3T_ready, t + 1)
            for tb in range(TB):
                last = nc.tensor.matmul(ps_tail[:, tb * P:(tb + 1) * P], x3T[:, tb * P:(tb + 1) * P], c_cb[:, :],
                                        start=True, stop=True)
            last.then_inc(cb_done, 1)

        def has(b):
            return not whole(b) or 0 <= b < NB

        def c_pe(b, u, p):
            for j in range(4):
                for g in range(GRP):
                    if has(b + 1):
                        c_m(b + 1, 1 - u, j, g)
                    if has(b):
                        c_x(b, u, j, g)
                    if (j, g) in USES[u]:
                        what, part, ahead = USES[u][j, g]
                        n = use(p, u, list(USES[u]).index((j, g)))
                        if wanted(p, what, ahead):
                            if what == "vt":
                                c_vt(p, part, n)
                            else:
                                c_project(p, what, part, n, ahead)
                    if g == 1:
                        if j == 0 and has(b):
                            c_t(b, 3)
                        if j > 0 and has(b + 1):
                            c_t(b + 1, j - 1)
                    if g == 2:
                        if j == 0 and has(b - 1):
                            c_pv(b - 1, 1 - u, p if u else p - 1, 3)
                        if j > 0 and has(b):
                            c_pv(b, u, p, j - 1)
                    if has(b - 1):
                        if (j, g) == (1, 0):
                            c_atr(b - 1, 1 - u, 0)
                        if (j, g) == (1, 2):
                            c_atr(b - 1, 1 - u, 1)
                        if (j, g) == (1, 3):
                            c_anT(b - 1)
                        if (j, g) == (2, 1):
                            c_wo_mm(b - 1)
                        if (j, g) == (3, 1):
                            c_x3T(b - 1)
                        if (j, g) == (3, 3):
                            c_linear(b - 1)

        def c_project_out(p, u, what, part, n, ahead):
            act = nc.scalar
            act.wait_ge(p_done, n + 1)
            k = "qkv".index(what)
            for i in range(4):
                c = 4 * part + i
                if what == "v":
                    dst = v_st[:, :, c, :]
                else:
                    par = (p + ahead) % 2
                    dst = qk_st[:, bass.ds(par, 1), :, k, c, :].rearrange("p o a i -> p (o a) i")
                last = act.activation(dst, ps_p[:, i * P:(i + 1) * P].rearrange("p (a i) -> p a i", a=8),
                                      ACT.Identity, bias=c_br[:, k, c:c + 1], scale=1.0)
            last.then_inc(p_ready, 1)

        def c_vt_out(b, p, part, n):
            act = nc.scalar
            act.wait_ge(p_done, n + 1)
            if part >= 2 and not (whole(b) and b == 0):
                act.wait_ge(pv_done, 4 * b)
            act.copy(vt[part // 2][:, 2 * (part % 2):2 * (part % 2) + 2].rearrange("p j k m -> p (j k m)"),
                     ps_p[:, :]).then_inc(p_ready, 1)

        def c_exp(b, j, g):
            act = nc.scalar
            act.wait_ge(x_done, 16 * b + 4 * j + g + 1)
            if g == 0 and not (whole(b) and 4 * b + j < 2):
                act.wait_ge(pv_done, 4 * b + j - 1)
            act.activation(pt[j % 2][:, g].rearrange("p k q -> p (k q)"), ps_x[g % 2][:, :], ACT.Exp,
                           scale=float(D1) ** -0.5).then_inc(p_exp_ready, 1)

        def c_aT_out(b, u, j):
            nc.scalar.wait_ge(pv_done, 4 * b + j + 1)
            nc.scalar.copy(aT[u][:, j, :].rearrange("p (i c) -> p c i", c=CH),
                           ps_pv[:, 0:S].rearrange("p (c i) -> p c i", c=CH)).then_inc(aT_ready, 1)

        def c_anT_out(t):
            nc.scalar.wait_ge(anT_done, t + 1)
            nc.scalar.copy(anT[:, :], ps_tail[:, 0:S]).then_inc(anT_ready, 1)

        def c_x3T_out(t):
            nc.scalar.wait_ge(x3T_done, t + 1)
            nc.scalar.copy(x3T[:, :], ps_tail[:, 0:S]).then_inc(x3T_ready, 1)

        def c_act(b, u, p):
            for j in range(4):
                for g in range(GRP):
                    if has(b):
                        c_exp(b, j, g)
                    if (j, g) in USES[u]:
                        what, part, ahead = USES[u][j, g]
                        n = use(p, u, list(USES[u]).index((j, g)))
                        if wanted(p, what, ahead):
                            if what == "vt":
                                c_vt_out(b, p, part, n)
                            else:
                                c_project_out(p, u, what, part, n, ahead)
                    if g == 3:
                        if j == 0 and has(b - 1):
                            c_aT_out(b - 1, 1 - u, 3)
                        if j > 0 and has(b):
                            c_aT_out(b, u, j - 1)
                    if has(b - 1):
                        if (j, g) == (2, 0):
                            c_anT_out(b - 1)
                        if (j, g) == (3, 2):
                            c_x3T_out(b - 1)

        def c_split(b, u, j):
            v = nc.vector
            n = 4 * b + j
            v.wait_ge(hi_ready, n + 1)
            if not (whole(b) and b < 2):
                v.wait_ge(x_done, 16 * (b - 2) + 4 * j + 4)
                v.wait_ge(k_alone_ready[j], 16 * GRP * (b - 1))
            par = (b // 2) % 2
            for k, dst in ((0, q_m), (1, k_m)):
                src = qk_st[:, bass.ds(par, 1), 4 * u + j, k].rearrange("p o c i -> p (o c i)")
                v.scalar_tensor_tensor(dst[u][:, j, :], qk_hi[j % 2][:, k, :].bitcast(FP32), c_low[:, k:k + 1],
                                       src, ALU.mult, ALU.add).then_inc(split_ready, 1)

        def c_max(b, j, g):
            v = nc.vector
            v.wait_ge(m_done, 16 * b + 4 * j + g + 1)
            v.tensor_reduce(mx[j % 2][:, :, g], ps_m[g % 2][:, :].rearrange("p (t k) -> p t k", t=TB), AX.X,
                            ALU.max).then_inc(mx_ready, 1)

        def c_pad(b, j):
            v = nc.vector
            n = 4 * b + j
            v.wait_ge(mx_ready, 4 * (n + 1))
            v.tensor_copy(mx_hi[:], mx[j % 2][:]).then_inc(mx_hi_ready, 1)
            v.wait_ge(mx_hi_ready, n + 1)
            if not (whole(b) and n == 0):
                v.wait_ge(t_done, n)
            v.tensor_copy(mx_pad[:, :, :, 0:19:18], mx_hi[:].bitcast(FP32).unsqueeze(3)
                          .broadcast_to([P, TB, GRP, 2])).then_inc(pad_set, 1)
            v.tensor_tensor(mx_pad[:, :, :, 9], mx[j % 2][:], mx_hi[:].bitcast(FP32),
                            ALU.subtract).then_inc(pad_set, 1)

        def c_q_x(b, u, j):
            v = nc.vector
            v.wait_ge(t_done, 4 * b + j + 1)
            v.tensor_tensor(q_x[u][:, j, :], ps_tr[:, 0:S], q_m[u][:, j, :].bitcast(FP32),
                            ALU.add).then_inc(q_x_ready, 1)

        def c_an(t, tb):
            v = nc.vector
            v.wait_ge(atr_done, 2 * t + tb + 1)
            heads = ps_tail[:, :].rearrange("p (h w) -> p h w", w=W32)
            v.reciprocal(den[:, tb, :], heads[:, :, 0]).then_inc(den_ready, 1)
            v.wait_ge(den_ready, 2 * t + tb + 1)
            if not (whole(t) and t == 0):
                v.wait_ge(anT_done, t)
            v.tensor_tensor(an[:, tb, :].rearrange("p (h d) -> p h d", d=D1), heads[:, :, 1:1 + D1],
                            den[:, tb, :].unsqueeze(2).broadcast_to([P, H1, D1]), ALU.mult).then_inc(an_ready, 1)

        def c_stats(i, t, y, ready):
            v = nc.vector
            v.wait_ge(ready, t + 1)
            for tb in range(TB):
                v.bn_stats(ln_st[i][:, tb, :], y[:, tb, :]).then_inc(ln_st_ready[i], 1)
            v.wait_ge(ln_st_ready[i], TB * (t + 1))
            own_wait()
            for tb in range(TB):
                v.bn_aggr(ln_mv[i][:, tb, :], ln_st[i][:, tb, :]).then_inc(ln_mv_ready[i], 1)

        def c_norm(i, t, y, dst, done):
            v = nc.vector
            v.wait_ge(ln_rs_ready[i], t + 1)
            for tb in range(TB):
                v.tensor_scalar(dst[:, tb, :], y[:, tb, :], ln_mv[i][:, tb, 0:1], ln_rs[i][:, tb:tb + 1],
                                ALU.subtract, ALU.mult).then_inc(done, 1)

        def c_y3(t):
            v = nc.vector
            v.wait_ge(wo_done, t + 1)
            v.wait_ge(xr3b_ready, t + 1)
            v.tensor_tensor(y3[:], ps_tail[:, 0:S].rearrange("p (t d) -> p t d", t=TB), xr3b[:],
                            ALU.add).then_inc(y3_ready, 1)

        def c_z(t):
            v = nc.vector
            v.wait_ge(cb_done, t + 1)
            v.tensor_tensor(z0[:], ps_tail[:, 0:S].rearrange("p (t d) -> p t d", t=TB),
                            c_scale[:].unsqueeze(1).broadcast_to([P, TB, D]), ALU.mult).then_inc(z0_ready, 1)
            v.wait_ge(z0_ready, t + 1)
            v.wait_ge(x3b_ready, t + 1)
            v.tensor_tensor(z1[:], z0[:], x3b[:], ALU.add).then_inc(z1_ready, 1)

        def c_dve(b, u, p):
            for j in range(4):
                for g in range(GRP):
                    if has(b + 1):
                        c_max(b + 1, j, g)
                    if g == 1:
                        if j == 0 and has(b):
                            c_q_x(b, u, 3)
                        if j > 0 and has(b + 1):
                            c_q_x(b + 1, 1 - u, j - 1)
                    if g == 0:
                        if j < 3 and has(b + 1):
                            c_split(b + 1, 1 - u, j + 1)
                        if j == 3 and has(b + 2):
                            c_split(b + 2, u, 0)
                    if g == 3 and has(b + 1):
                        c_pad(b + 1, j)
                    if has(b - 2):
                        if (j, g) == (0, 0):
                            c_z(b - 2)
                        if (j, g) == (0, 1):
                            c_stats(1, b - 2, z1, z1_ready)
                        if (j, g) == (0, 3):
                            if not (whole(b) and b == 2):
                                nc.vector.wait_ge(out_stored, 16 * (b - 2))
                            c_norm(1, b - 2, z1, res, res_ready)
                    if has(b - 1):
                        if (j, g) == (1, 1):
                            c_an(b - 1, 0)
                        if (j, g) == (1, 2):
                            c_an(b - 1, 1)
                        if (j, g) == (2, 1):
                            c_y3(b - 1)
                        if (j, g) == (2, 2):
                            c_stats(0, b - 1, y3, y3_ready)
                        if (j, g) == (3, 0):
                            c_norm(0, b - 1, y3, x3s, x3_ready)

        def c_hi(b, u, j):
            po = nc.gpsimd
            n = 4 * b + j
            po.wait_ge(p_ready, 16 * (b // 2) + 8)
            if not (whole(b) and n < 2):
                po.wait_ge(split_ready, 2 * (n - 1))
            par = (b // 2) % 2
            po.tensor_tensor(qk_hi[j % 2][:].rearrange("p k q -> p (k q)"),
                             qk_st[:, bass.ds(par, 1), 4 * u + j].rearrange("p o k c i -> p (o k c i)"),
                             one[:, 0:1].broadcast_to([P, 2 * S]), ALU.mult).then_inc(hi_ready, 1)

        def c_rs(i, t):
            po = nc.gpsimd
            po.wait_ge(ln_mv_ready[i], TB * (t + 1))
            po.tensor_tensor(ln_ve[i][:, :], ln_mv[i][:, :, 1], eps[:, 0:TB], ALU.add).then_inc(ln_ve_ready[i], 1)
            po.wait_ge(ln_ve_ready[i], t + 1)
            po.tensor_tensor(ln_rs[i][:, :], ln_ve[i][:, :], minus_half[:, 0:TB], ALU.pow).then_inc(ln_rs_ready[i], 1)

        def c_xr3b(t):
            po = nc.gpsimd
            po.wait_ge(xr3_loaded, 16 * (t + 1))
            if not (whole(t) and t == 0):
                po.wait_ge(y3_ready, t)
            po.tensor_tensor(xr3b[:], xr3[:], c_bo[:].unsqueeze(1).broadcast_to([P, TB, D]),
                             ALU.add).then_inc(xr3b_ready, 1)

        def c_x3b(t):
            po = nc.gpsimd
            po.wait_ge(x3_ready, TB * (t + 1))
            if not (whole(t) and t == 0):
                po.wait_ge(z1_ready, t)
            po.tensor_tensor(x3b[:], x3s[:], c_fb[:].unsqueeze(1).broadcast_to([P, TB, D]),
                             ALU.add).then_inc(x3b_ready, 1)

        def c_pool(b, u, p):
            for j in range(4):
                if j < 2 and has(b + 1):
                    c_hi(b + 1, 1 - u, j + 2)
                if j >= 2 and has(b + 2):
                    c_hi(b + 2, u, j - 2)
                if j == 0 and has(b - 2):
                    c_rs(1, b - 2)
                if has(b - 1):
                    if j == 1:
                        c_xr3b(b - 1)
                    if j == 2:
                        c_rs(0, b - 1)
                    if j == 3:
                        c_x3b(b - 1)

        def c_load_kv(p):
            if not (whole(p) and p < 1):
                nc.sync.wait_ge(p_done, use(p - 2, 1, 3))
            nc.sync.dma_start(x_kv[:, :], x2T_d[:, bass.ds(p * 2 * S, 2 * S)]).then_inc(x_kv_loaded, 16)

        def c_load_q(p):
            if not (whole(p) and p < 1):
                nc.sync.wait_ge(p_done, 4 if whole(p) and p == 1 else use(p - 3, 1, 6))
            nc.sync.dma_start(x_q[:, :], x2T_d[:, bass.ds(p * 2 * S, 2 * S)]).then_inc(x_q_loaded, 16)

        def c_load_res(t):
            if not (whole(t) and t == 0):
                nc.sync.wait_ge(xr3b_ready, t)
            nc.sync.dma_start(xr3[:], x2_d.rearrange("(n p) d -> p n d", p=P)[:, bass.ds(t * TB, TB), :]
                              ).then_inc(xr3_loaded, 16)

        def c_store(t):
            nc.sync.wait_ge(res_ready, TB * (t + 1))
            nc.sync.dma_start(t_out.rearrange("(n p) d -> p n d", p=P)[:, bass.ds(t * TB, TB), :],
                              res[:]).then_inc(out_stored, 16)

        def c_k_alone(b, u, j):
            nc.sync.wait_ge(split_ready, 2 * (4 * b + j + 1))
            for g in range(GRP):
                lo = W32 * g
                nc.sync.dma_start(k_alone[u][lo:lo + W32, j, g, :].bitcast(FP32),
                                  k_m[u][lo:lo + W32, j, :].bitcast(FP32)).then_inc(k_alone_ready[j], 16)

        def c_sp(b, u, p):
            if has(b + 1):
                c_k_alone(b + 1, 1 - u, 1)
            if has(b - 1):
                c_load_res(b - 1)
            if u == 0 and wanted(p, "q", 2):
                c_load_q(p + 2)
            if has(b + 1):
                c_k_alone(b + 1, 1 - u, 2)
            if has(b - 2):
                c_store(b - 2)
            if u == 1 and wanted(p, "v", 2):
                c_load_kv(p + 2)
            if has(b + 1):
                c_k_alone(b + 1, 1 - u, 3)
            if has(b + 2):
                c_k_alone(b + 2, u, 0)

        def c_sp_consts():
            sp = nc.sync
            loads = [(c_w[0], "c_wq"), (c_w[1], "c_wk"), (c_w[2], "c_wv"), (c_ws[0], "c_wqs"), (c_ws[1], "c_wks")]
            for dst, name in loads:
                sp.dma_start(dst[:].rearrange("p c w -> p (c w)"), t[name]).then_inc(c_loaded, 16)
            sp.dma_start(c_b[:].rearrange("p k c -> p (k c)"), t["c_b"]).then_inc(c_loaded, 16)
            sp.dma_start(c_bs[:].rearrange("p k c -> p (k c)"), t["c_bs"]).then_inc(c_loaded, 16)
            for dst, name in [(c_cos, "c_cos"), (c_sin, "c_sin"), (c_sgn, "c_sgn")]:
                sp.dma_start(dst[:, :], t[name].broadcast_to([P, W32])).then_inc(c_loaded, 16)
            for dst, name in [(c_bo, "c_bo"), (c_scb, "c_scb"), (c_fb, "c_fb")]:
                sp.dma_start(dst[:, :], t[name].broadcast_to([P, D])).then_inc(c_loaded, 16)
            for dst, name in [(c_cosp, "c_cosp"), (c_sinp, "c_sinp"), (c_sgnp, "c_sgnp"), (c_spec, "c_spec"),
                              (c_low, "c_low"), (c_wo, "c_wo"), (c_cb, "c_cb")]:
                sp.dma_start(dst[:, :], t[name]).then_inc(c_loaded, 16)
            return len(loads) + 2 + 3 + 3 + 7

        def c_prepare():
            v = nc.vector
            v.wait_ge(c_loaded, 16 * 20)
            v.memset(mx_pad[:], 0.0).then_inc(pad_ready, 1)
            v.tensor_tensor(c_sins[:], c_sin[:], c_sgn[:], ALU.mult).then_inc(c_prep, 1)
            v.tensor_tensor(c_sinsp[:], c_sinp[:], c_sgnp[:], ALU.mult).then_inc(c_prep, 1)
            v.tensor_scalar(c_scale[:], c_scb[:], 1.0 / 127.0, None, ALU.mult).then_inc(c_prep, 1)
            v.wait_ge(c_prep, 3)
            wide = lambda a: a[:].unsqueeze(1).broadcast_to([P, CH, W32])
            for k in range(2):
                v.tensor_tensor(c_wt[2 * k][:], c_w[k][:], wide(c_cos), ALU.mult).then_inc(c_prep, 1)
                v.tensor_tensor(c_wt[2 * k + 1][:], c_ws[k][:], wide(c_sins), ALU.mult).then_inc(c_prep, 1)
                v.tensor_scalar(c_bt[:, 2 * k], c_b[:, k], c_cosp[:, 0:1], None, ALU.mult).then_inc(c_prep, 1)
                v.tensor_scalar(c_bt[:, 2 * k + 1], c_bs[:, k], c_sinsp[:, 0:1], None, ALU.mult).then_inc(c_prep, 1)
            v.wait_ge(c_prep, 11)
            for k in range(2):
                v.tensor_tensor(c_wr[k][:], c_wt[2 * k][:], c_wt[2 * k + 1][:], ALU.add).then_inc(c_prep, 1)
                v.scalar_tensor_tensor(c_br[:, k], c_bt[:, 2 * k], c_spec[:, k:k + 1], c_bt[:, 2 * k + 1],
                                       ALU.add, ALU.add).then_inc(c_prep, 1)
            v.tensor_scalar(c_br[:, 2], c_b[:, 2], c_spec[:, 2:3], None, ALU.add).then_inc(c_prep, 1)
            for k in k_alone:
                v.memset(k[:].bitcast(FP32), 0.0).then_inc(alone_zeroed, 1)

        C_PREP = 16

        def c_loop(eng, body):
            body(-1, 1, -1)
            body(0, 0, 0)
            body(1, 1, 0)
            with eng.Fori(1, NPAIR - 2) as p:
                body(p * 2, 0, p)
                body(p * 2 + 1, 1, p)
            for p in range(NPAIR - 2, NPAIR + 1):
                for u in range(2):
                    body(2 * p + u, u, p)

        @block.sync
        def _(sp):
            a_consts = [(wv, t["wvT"]), (wq, t["wqT"]), (wk, t["wkT"]), (qb, t["qbT"]), (kb_, t["kbT"]),
                        (vb, t["vb"].broadcast_to([P, H0 * P0])), (lb, t["lb"].broadcast_to([P, D])),
                        (gate_b, t["gate_b"].broadcast_to([P, E])), (gate_w, t["gate_wT"]),
                        (tri, t["tri"].unsqueeze(0).broadcast_to([P, NG, NG])), (ident, t["ident"]),
                        (lw, t["lwT"].rearrange("(j p) d -> p j d", p=P))]
            sp.dma_start(xv[:, :], t["xT"][:, 0:S]).then_inc(xv_loaded, 16)
            for dst, src in a_consts:
                sp.dma_start(dst[:], src).then_inc(consts, 16)
            sp.dma_start(xT[:, :], t["xT"]).then_inc(x_all, 16)
            x_t = t["x"].rearrange("(n p) d -> p n d", p=P)
            sp.dma_start(xr[:], x_t[:, 0:TB, :]).then_inc(xr_loaded, 16)
            a_sp_batch(0, True, True, False)
            a_sp_batch(1, False, True, False)
            with sp.Fori(2, NB - 1) as b:
                a_sp_batch(b, False, False, False)
            a_sp_batch(NB - 1, False, False, True)
            a_store_x1(NB - 1)
            a_store_rwT(NB - 2)
            a_store_rwT(NB - 1)
            b_sp()
            sp.wait_ge(x2_stored, 16 * NTILE)
            sp.wait_ge(x2T_stored, 16 * NTILE)
            c_sp_consts()
            c_load_q(0)
            c_load_kv(0)
            c_load_q(1)
            sp.wait_ge(alone_zeroed, 2)
            c_k_alone(0, 0, 0)
            c_loop(sp, c_sp)
            sp.wait_ge(out_stored, 16 * NB)

        @block.tensor
        def _(pe):
            pe.wait_ge(consts, 16 * 12)
            pe.wait_ge(x_all, 16)
            pe.wait_ge(zeros_ready, 4)
            a_v_part(0, 0, 0)
            a_qk(0, 0)
            a_v_part(0, 0, 1)
            a_qk(0, 1)
            a_scores(0, 0)
            a_pe_batch(0, True, True, False)
            a_pe_batch(1, False, True, False)
            with pe.Fori(2, NB - 1) as b:
                a_pe_batch(b, False, False, False)
            a_pe_batch(NB - 1, False, False, True)
            a_pv(NB - 1, NJ - 1)
            a_out(NB - 1)
            a_x1T(NB - 1)
            a_logits(NB - 1, 4 * NB)
            a_rwT(NB - 2, 4 * NB, NB)
            a_rwT(NB - 1, 4 * NB, NB)
            pe.wait_ge(rwT_ready, NB)
            pe.wait_ge(w_hi_loaded, 32)
            b_pe_tile(0, 0, True)
            with pe.Fori(0, NTILE // 2 - 1) as k:
                n = k * 2 + 1
                b_pe_tile(n, 1, False)
                b_pe_tile(n + 1, 0, False)
            b_pe_tile(NTILE - 1, 1, False)
            b_down(NTILE - 1, NC - 2)
            b_down(NTILE - 1, NC - 1)
            b_oT(NTILE - 1)
            b_x2T(NTILE - 1)
            pe.wait_ge(c_prep, C_PREP)
            pe.wait_ge(x2T_ready, NTILE)
            for n, (what, part, ahead) in enumerate(START):
                c_project(-1, what, part, n, ahead)
            c_loop(pe, c_pe)

        @block.scalar
        def _(act):
            act.wait_ge(consts, 16 * 12)
            act.mul(qb8[:, :], qb[:, :], 0.125).then_inc(qb8_ready, 1)
            act.wait_ge(qb8_ready, 1)
            a_qk_out(0, 0)
            a_qk_out(0, 1)
            a_exp(0, 0)
            a_act_batch(0, True, True, False)
            a_act_batch(1, False, True, False)
            with act.Fori(2, NB - 1) as b:
                a_act_batch(b, False, False, False)
            a_act_batch(NB - 1, False, False, True)
            a_x1T_out(NB - 1)
            a_r_exp(NB - 1)
            a_rwT_out(NB - 2)
            a_rwT_out(NB - 1)
            act.wait_ge(rwT_stored, 16 * NB)
            b_x_hi(0, 0)
            b_act_tile(0, 0, True, False)
            with act.Fori(0, NTILE // 2 - 1) as k:
                n = k * 2 + 1
                b_act_tile(n, 1, False, False)
                b_act_tile(n + 1, 0, False, False)
            b_act_tile(NTILE - 1, 1, False, True)
            b_h_hi(NTILE - 1, NC - 1)
            b_oT_out(NTILE - 1)
            b_x2T_out(NTILE - 1)
            act.wait_ge(c_prep, C_PREP)
            for n, (what, part, ahead) in enumerate(START):
                c_project_out(-1, 0, what, part, n, ahead)
            c_loop(act, c_act)

        @block.vector
        def _(dve):
            for q in q_sb:
                for h in range(2):
                    lo = (1 - h) * P0
                    dve.memset(q[lo:lo + P0, h, :], 0.0).then_inc(zeros_ready, 1)
            dve.wait_ge(consts, 16 * 12)
            a_v_out(0, 0, 0)
            a_v_out(0, 0, 1)
            a_max(0, 0)
            a_dve_batch(0, True, True, False)
            a_dve_batch(1, False, True, False)
            with dve.Fori(2, NB - 1) as b:
                a_dve_batch(b, False, False, False)
            a_dve_batch(NB - 1, False, False, True)
            a_c_out(NB - 1, NJ - 1)
            a_y(NB - 1)
            route_groups(NB - 2)
            a_norm(NB - 1)
            route_best_eight(NB - 2)
            route_weights(NB - 2)
            route_scores(NB - 1)
            route_best_two(NB - 1)
            route_groups(NB - 1)
            route_best_eight(NB - 1)
            route_weights(NB - 1)
            dve.wait_ge(rwT_stored, 16 * NB)
            dve.wait_ge(w_hi_loaded, 32)
            b_lo(0)
            b_lo(1)
            b_dve_tile(0, True)
            with dve.Fori(0, NTILE // 2 - 1) as k:
                n = k * 2 + 1
                b_dve_tile(n, False)
                b_dve_tile(n + 1, False)
            b_dve_tile(NTILE - 1, False)
            b_y(NTILE - 1)
            b_stats(NTILE - 1)
            b_mv(NTILE - 1)
            b_norm(NTILE - 1, range(SUB))
            c_prepare()
            c_split(0, 0, 0)
            c_loop(dve, c_dve)

        @block.gpsimd
        def _(pool):
            pool.memset(minus_half[:, :], -0.5).then_inc(const_ready, 1)
            pool.memset(eps[:, :], EPS).then_inc(const_ready, 1)
            pool.memset(one[:, :], 1.0).then_inc(const_ready, 1)
            pool.wait_ge(const_ready, 3)
            pool.wait_ge(consts, 16 * 12)
            a_pool_batch(0, True, True, False)
            pool.dma_start(w_hi[:], t["w_all"].rearrange("p (c a m) -> p c a m", a=3, m=P)).then_inc(w_hi_loaded, 16)
            pool.dma_start(select[:], t["select"].rearrange("p (c m) -> p c m", m=P)).then_inc(w_hi_loaded, 16)
            a_pool_batch(1, False, True, False)
            with pool.Fori(2, NB - 1) as b:
                a_pool_batch(b, False, False, False)
            a_pool_batch(NB - 1, False, False, True)
            a_rstd(NB - 1)
            pool.wait_ge(rwT_stored, 16 * NB)
            b_x_lo(0, 0)
            b_pool_tile(0, 0, True, False)
            with pool.Fori(0, NTILE // 2 - 1) as k:
                n = k * 2 + 1
                b_pool_tile(n, 1, False, False)
                b_pool_tile(n + 1, 0, False, False)
            b_pool_tile(NTILE - 1, 1, False, True)
            b_rstd(NTILE - 1)
            c_hi(0, 0, 0)
            c_hi(0, 0, 1)
            c_loop(pool, c_pool)


def blocks(routed, shared):
    import numpy as np
    pad = np.zeros((NC * P - FF, D), np.float32)
    return np.concatenate([routed.reshape(E * I, D), shared, pad]).reshape(NC, P, D)


def chunked(w, times):
    import numpy as np
    out = np.zeros((P, CH, W32), np.float32)
    for k in range(times):
        out[:, :, 9 * k + 1:9 * k + 9] = w.T.reshape(D, CH, D1)
    return out.reshape(P, CH * W32)


def chunked_bias(b, times):
    import numpy as np
    out = np.zeros((GRP, W32, CH), np.float32)
    for k in range(times):
        out[:, 9 * k + 1:9 * k + 9, :] = b.reshape(CH, D1).T
    return out.reshape(P, CH)


def tripled(v8):
    import numpy as np
    out = np.zeros(W32, np.float32)
    for k in range(3):
        out[9 * k + 1:9 * k + 9] = v8
    return out


def partner(a):
    return a.reshape(a.shape[0] // 2, 2, -1)[:, ::-1].reshape(a.shape)


def layout(v):
    import numpy as np
    x = v["L0_attn_x"].reshape(TOK, D)
    heads = lambda w: w.reshape(H0 * P0, D).T
    gate = blocks(v["L0_ffn_Wg"], v["L0_ffn_Sg"]).transpose(2, 0, 1)
    up = blocks(v["L0_ffn_Wu"], v["L0_ffn_Su"]).transpose(2, 0, 1)
    down = blocks(v["L0_ffn_Wd"].transpose(0, 2, 1), v["L0_ffn_Sd"].T).transpose(1, 0, 2)
    belongs = (np.arange(E * I)[None] // I == np.arange(E)[:, None]).astype(np.float32)
    wq, wk, wv, bq, bk, bv = (v["L1_attn_" + n] for n in ("wq", "wk", "wv", "bq", "bk", "bv"))
    cos = tripled(np.repeat(v["L1_attn_rot_cos"][S], 2))
    sin = tripled(np.repeat(v["L1_attn_rot_sin"][S], 2))
    sign = tripled(np.tile(np.float32([-1, 1]), D1 // 2))
    spec = np.zeros((GRP, W32, 3), np.float32)
    spec[:, 0:19:9, 1] = -1
    spec[:, 0, 2] = 1
    low = np.zeros((GRP, W32, 2), np.float32)
    low[:, 9:18, 0] = -1
    low[:, 18:27, 1] = -1
    return dict(
        x=x, xT=x.T, wqT=heads(v["L0_attn_q_w"]), wkT=heads(v["L0_attn_k_w"]), wvT=heads(v["L0_attn_v_w"]),
        qbT=v["L0_attn_q_b"].reshape(NJ, P).T, kbT=v["L0_attn_k_b"].reshape(NJ, P).T,
        vb=v["L0_attn_v_b"].reshape(1, H0 * P0), lb=v["L0_attn_l_b"].reshape(1, D), lwT=v["L0_attn_l_w"].T,
        gate_b=v["L0_ffn_gate_bias"].reshape(1, E), gate_wT=v["L0_ffn_gate_w"].T,
        tri=np.tril(np.ones((NG, NG), np.float32), -1), ident=np.eye(P, dtype=np.float32),
        w_all=np.stack([gate, up, down], 2).reshape(P, NC * 3 * P), select=np.concatenate([belongs, belongs]),
        c_wq=chunked(wq, 3), c_wk=chunked(wk, 3), c_wv=chunked(wv, 1),
        c_wqs=chunked(partner(wq), 3), c_wks=chunked(partner(wk), 3),
        c_b=np.stack([chunked_bias(bq, 3), chunked_bias(bk, 3), chunked_bias(bv, 1)], 1).reshape(P, 3 * CH),
        c_bs=np.stack([chunked_bias(partner(bq), 3), chunked_bias(partner(bk), 3)], 1).reshape(P, 2 * CH),
        c_cos=cos[None], c_sin=sin[None], c_sgn=sign[None],
        c_cosp=np.tile(cos, GRP)[:, None], c_sinp=np.tile(sin, GRP)[:, None], c_sgnp=np.tile(sign, GRP)[:, None],
        c_spec=spec.reshape(P, 3), c_low=low.reshape(P, 2), c_wo=v["L1_attn_wo"].T, c_bo=v["L1_attn_bo"][None],
        c_cb=v["L1_ffn_CB"].T, c_scb=v["L1_ffn_SCB"][None], c_fb=v["L1_ffn_bias"][None])


def kernel(**inputs):
    import numpy as np
    from concourse import bacc
    from concourse.bass_utils import run_bass_kernel_spmd

    nc = bacc.Bacc("TRN2", target_bir_lowering=False, num_devices=1)
    laid = {k: np.ascontiguousarray(a) for k, a in layout({k: np.asarray(a) for k, a in inputs.items()}).items()}
    t = {k: nc.dram_tensor(f"in_{k}_dram", a.shape, mybir.dt.from_np(a.dtype), kind="ExternalInput").ap()
         for k, a in laid.items()}
    t["out"] = nc.dram_tensor("out_0_dram", (TOK, D), FP32, kind="ExternalOutput").ap()
    build(nc, t)
    result = run_bass_kernel_spmd(nc, [{f"in_{k}_dram": a for k, a in laid.items()}], core_ids=[0])
    return result.results[0]["out_0_dram"].reshape(NB, S, D)
```

```python
import concourse.bass as bass
from concourse import mybir
from contextlib import ExitStack

FP32 = mybir.dt.float32
F32R = mybir.dt.float32r
ALU = mybir.AluOpType
ACT = mybir.ActivationFunctionType
AX = mybir.AxisListType

P = 128
NB, S, D = 16, 256, 128
TOK = NB * S
NT = TOK // P
TB = S // P
EPS = 1e-5

H0, P0 = 16, 64
NJ = H0 // 2

E, I = 64, 88
NG, GE = 8, 8
KEEP_GROUPS = 4
ROUTED_SCALE = 2.5
FF = E * I + 2 * I
NC = (FF + P - 1) // P
NCR = E * I // P
TILE = 512
NTILE = TOK // TILE
SUB = TILE // P
FAR = 3.0e38

H1, D1 = 16, 8
CH = D // D1
HT = S // H1
GRP = 4
W32 = 32
C_PARTS = [CH * W32] * 5 + [3 * CH, 2 * CH] + [W32] * 3 + [1, 1, 1, 3, 2]
C_EARLY = sum(C_PARTS)


def build(nc, t):
    t_out = t["out"]
    with ExitStack() as ctx:
        def sb(name, shape, dt=FP32, stage=ctx):
            return stage.enter_context(nc.sbuf_tensor(name, shape, dt))

        def sem(name):
            return ctx.enter_context(nc.semaphore(name))

        bank = [ctx.enter_context(nc.psum_tensor(f"bank{i}", [P, 512], FP32)) for i in range(8)]

        x1_d = nc.dram_tensor("x1_d", [TOK, D], FP32, kind="Internal").ap()
        x1T_d = nc.dram_tensor("x1T_d", [D, TOK], FP32, kind="Internal").ap()
        rwT_d = nc.dram_tensor("rwT_d", [P, TOK], FP32, kind="Internal").ap()
        x2_d = nc.dram_tensor("x2_d", [TOK, D], FP32, kind="Internal").ap()
        x2T_d = nc.dram_tensor("x2T_d", [D, TOK], FP32, kind="Internal").ap()

        ident = sb("ident", [P, P])
        minus_half = sb("minus_half", [P, 4])
        eps = sb("eps", [P, 4])
        one = sb("one", [P, 1])
        waited = sb("waited", [P, 1])
        st6 = sb("st6", [P, SUB, 6])
        mv = sb("mv", [P, SUB, 2])
        veps = sb("veps", [P, SUB])
        rstd = sb("rstd", [P, SUB])

        st_w = ExitStack()
        ctx_sb = sb
        sb = lambda name, shape, dt=FP32: ctx_sb(name, shape, dt, st_w)
        w_hi = sb("w_hi", [P, NC, 3, P], F32R)
        w_raw = sb("w_raw", [P, 2, 3, P])
        select = sb("select", [P, NCR, P], F32R)
        xf = sb("xf", [P, TILE])
        rw_in = [sb(f"rw_in{i}", [P, TILE], F32R) for i in range(2)]
        xres = sb("xres", [P, SUB, D])

        st_a = ExitStack()
        sb = lambda name, shape, dt=FP32: ctx_sb(name, shape, dt, st_a)
        a_w_all = sb("a_w_all", [P, 3, H0 * P0])
        a_w = [a_w_all[:, i] for i in range(3)]
        a_w_hi = [sb(f"a_w_hi{i}", [P, H0 * P0], F32R) for i in range(3)]
        a_w_lo = [sb(f"a_w_lo{i}", [P, H0 * P0], F32R) for i in range(3)]
        lw = sb("lw", [P, NJ, D])
        qb = sb("qb", [P, NJ])
        qb8 = sb("qb8", [P, NJ])
        kb_ = sb("kb", [P, NJ])
        vb = sb("vb", [P, H0 * P0])
        lb = sb("lb", [P, D])
        gate_w = sb("gate_w", [P, E])
        gate_b = sb("gate_b", [P, E])
        tri = sb("tri", [P, NG, NG])
        xv = sb("xv", [P, S])
        xv_half = sb("xv_half", [P, 2, S], F32R)
        xq_half = sb("xq_half", [P, 2, 2, S], F32R)
        xr = sb("xr", [P, TB, D])
        xrl = sb("xrl", [P, TB, D])
        v_sb = sb("v_sb", [P, TB, H0 * P0])
        q_hi = [sb(f"q_hi{i}", [P, S], F32R) for i in range(2)]
        q_lo = [sb(f"q_lo{i}", [P, S], F32R) for i in range(2)]
        k_hi = [sb(f"k_hi{i}", [P, S], F32R) for i in range(2)]
        k_lo = [sb(f"k_lo{i}", [P, S], F32R) for i in range(2)]
        e_sb = [sb(f"e_sb{i}", [P, 2, TB, S]) for i in range(2)]
        vn_sb = [sb(f"vn_sb{i}", [P, TB, 2, P0]) for i in range(2)]
        nmax = sb("nmax", [P, NJ, TB, 2])
        esum = sb("esum", [P, NJ, TB, 2])
        erec = sb("erec", [P, NJ, TB, 2])
        ctxT = a_w_all[:].rearrange("p i c -> p (i c)")[:, 0:NJ * S].rearrange("p (j s) -> p j s", j=NJ)
        y_sb = sb("y_sb", [P, TB, D])
        rwTs = sb("rwTs", [P, S], F32R)
        x1s = sb("x1s", [P, TB, D])
        x1Ts = sb("x1Ts", [P, S])
        r_exp = sb("r_exp", [P, TB, E])
        r_one = sb("r_one", [P, TB, E])
        score = sb("score", [P, TB, E])
        choice = sb("choice", [P, TB, E])
        top = sb("top", [P, TB, NG, 8])
        gsum = sb("gsum", [P, TB, NG])
        g_gt = sb("g_gt", [P, TB, NG, NG])
        g_eq = sb("g_eq", [P, TB, NG, NG])
        g_tie = sb("g_tie", [P, TB, NG, NG])
        g_cnt = sb("g_cnt", [P, TB, NG, NG])
        rank = sb("rank", [P, TB, NG])
        gmask = sb("gmask", [P, TB, NG])
        masked = sb("masked", [P, TB, E])
        masked0 = sb("masked0", [P, TB, E])
        top8 = sb("top8", [P, TB, 8])
        marked = sb("marked", [P, TB, E])
        sel = sb("sel", [P, TB, E])
        wsel = sb("wsel", [P, TB, E])
        wsum = sb("wsum", [P, TB])
        wsum2 = sb("wsum2", [P, TB])
        wrec = sb("wrec", [P, TB])
        wrec2 = sb("wrec2", [P, TB])
        rw = sb("rw", [P, TB, E])
        rw_hi = sb("rw_hi", [P, TB, E], F32R)
        rw_st = sb("rw_st", [P, TB, 2, E])
        st_a.close()
        sb = ctx_sb

        st_b = ExitStack()
        sb = lambda name, shape, dt=FP32: ctx_sb(name, shape, dt, st_b)
        w_lo = sb("w_lo", [P, NC, 3, P], F32R)
        x_hi = [sb(f"x_hi{i}", [P, TILE], F32R) for i in range(2)]
        x_lo = [sb(f"x_lo{i}", [P, TILE], F32R) for i in range(2)]
        sg = [sb(f"sg{i}", [P, TILE]) for i in range(2)]
        hf = [sb(f"hf{i}", [P, TILE]) for i in range(2)]
        h_hi = [sb(f"h_hi{i}", [P, TILE], F32R) for i in range(2)]
        h_lo = [sb(f"h_lo{i}", [P, TILE], F32R) for i in range(2)]
        oT = sb("oT", [P, TILE])
        y2 = sb("y2", [P, SUB, D])
        x2s = sb("x2s", [P, SUB, D])
        x2Ts = sb("x2Ts", [P, TILE])
        st_b.close()
        st_w.close()
        sb = ctx_sb

        st_c = ExitStack()
        sb = lambda name, shape, dt=FP32: ctx_sb(name, shape, dt, st_c)
        c_early = sb("c_early", [P, C_EARLY])
        c_late = sb("c_late", [P, 5, D])
        parts, at = [], 0
        for width in C_PARTS:
            parts.append(c_early[:, at:at + width])
            at += width
        chunks = lambda a: a.rearrange("p (c w) -> p c w", c=CH)
        c_w = [chunks(a) for a in parts[0:3]]
        c_ws = [chunks(a) for a in parts[3:5]]
        c_b = parts[5].rearrange("p (k c) -> p k c", k=3)
        c_bs = parts[6].rearrange("p (k c) -> p k c", k=2)
        c_cos, c_sin, c_sgn, c_cosp, c_sinp, c_sgnp, c_spec = parts[7:14]
        c_low = parts[14]
        c_wo, c_cb, c_bo, c_scb, c_fb = (c_late[:, i, :] for i in range(5))
        c_wt = [sb(f"c_wt{i}", [P, CH, W32]) for i in range(4)]
        c_wr = [sb(f"c_wr{i}", [P, CH, W32]) for i in range(2)]
        c_bt = sb("c_bt", [P, 4, CH])
        c_br = sb("c_br", [P, 3, CH])
        c_sins = sb("c_sins", [P, W32])
        c_sinsp = sb("c_sinsp", [P, 1])
        c_scale = sb("c_scale", [P, D])
        x_kv = sb("x_kv", [P, 2 * S])
        x_q = sb("x_q", [P, 2 * S])
        mx_pad = sb("mx_pad", [P, TB, GRP, W32])
        k_alone = [sb(f"k_alone{i}", [P, 4, GRP, S], F32R) for i in range(2)]
        qk_st = sb("qk_st", [P, 2, 8, 2, CH, HT])
        v_st = sb("v_st", [P, 8, CH, HT])
        qk_hi = [sb(f"qk_hi{i}", [P, 2, S], F32R) for i in range(2)]
        q_m = [sb(f"q_m{i}", [P, 4, S], F32R) for i in range(2)]
        k_m = [sb(f"k_m{i}", [P, 4, S], F32R) for i in range(2)]
        q_x = [sb(f"q_x{i}", [P, 4, S], F32R) for i in range(2)]
        mx = [sb(f"mx{i}", [P, TB, GRP]) for i in range(2)]
        mx_hi = sb("mx_hi", [P, TB, GRP], F32R)
        vt = [sb(f"vt{i}", [P, 4, TB, P]) for i in range(2)]
        pt = [sb(f"pt{i}", [P, GRP, TB, S]) for i in range(2)]
        aT = [sb(f"aT{i}", [P, 4, S]) for i in range(2)]
        den = sb("den", [P, TB, H1])
        an = sb("an", [P, TB, D])
        anT = sb("anT", [P, S])
        xr3 = sb("xr3", [P, TB, D])
        xr3b = sb("xr3b", [P, TB, D])
        y3 = sb("y3", [P, TB, D])
        x3s = sb("x3s", [P, TB, D])
        x3b = sb("x3b", [P, TB, D])
        x3T = sb("x3T", [P, S])
        z0 = sb("z0", [P, TB, D])
        z1 = sb("z1", [P, TB, D])
        res = sb("res", [P, TB, D])
        ln_st = [sb(f"ln_st{i}", [P, TB, 6]) for i in range(2)]
        ln_mv = [sb(f"ln_mv{i}", [P, TB, 2]) for i in range(2)]
        ln_ve = [sb(f"ln_ve{i}", [P, TB]) for i in range(2)]
        ln_rs = [sb(f"ln_rs{i}", [P, TB]) for i in range(2)]
        st_c.close()
        sb = ctx_sb

        ps_qk, ps_s, ps_c, ps_v = (bank[0], bank[7]), bank[1:5], bank[5], bank[6]

        consts = sem("consts")
        early_consts = sem("early_consts")
        w_loaded = [sem(f"w_loaded{i}") for i in range(3)]
        const_ready = sem("const_ready")
        a_w_hi_ready = sem("a_w_hi_ready")
        a_w_lo_ready = sem("a_w_lo_ready")
        xv_hi_ready = sem("xv_hi_ready")
        xv_lo_ready = sem("xv_lo_ready")
        xq_copied = sem("xq_copied")
        qk_lo_ready = sem("qk_lo_ready")
        xv_loaded = sem("xv_loaded")
        xr_loaded = sem("xr_loaded")
        xrl_ready = sem("xrl_ready")
        qb8_ready = sem("qb8_ready")
        v_done = sem("v_done")
        v_ready = sem("v_ready")
        qk_done = sem("qk_done")
        qk_ready = sem("qk_ready")
        s_done = sem("s_done")
        max_ready = sem("max_ready")
        e_ready = sem("e_ready")
        rec_ready = sem("rec_ready")
        vn_ready = sem("vn_ready")
        c_done = sem("c_done")
        c_ready = sem("c_ready")
        o_done = sem("o_done")
        y_ready = sem("y_ready")
        stats_ready = sem("stats_ready")
        mv_ready = sem("mv_ready")
        veps_ready = sem("veps_ready")
        rstd_ready = sem("rstd_ready")
        x1_ready = sem("x1_ready")
        x1_stored = sem("x1_stored")
        x1T_done = sem("x1T_done")
        x1T_ready = sem("x1T_ready")
        x1T_stored = sem("x1T_stored")
        rwT_stored = sem("rwT_stored")
        logit_done = sem("logit_done")
        r_exp_ready = sem("r_exp_ready")
        rt = sem("rt")
        rw_ready = sem("rw_ready")
        rwT_done = sem("rwT_done")
        rwT_ready = sem("rwT_ready")
        block = ctx.enter_context(nc.Block())

        def own_wait():
            nc.vector.memset(waited[:, :], 0.0)


        def a_v_part(b, half, kb):
            n = 2 * half + kb
            pe = nc.tensor
            if not (isinstance(b, int) and b == 0 and n == 0):
                pe.wait_ge(v_ready, 4 * b + n)
            if n == 0 and not (isinstance(b, int) and b < 2):
                pe.wait_ge(r_exp_ready, b - 1)
            if n == 2 and not (isinstance(b, int) and b < 1):
                pe.wait_ge(y_ready, b)
            if kb == 0 and half == 0:
                pe.wait_ge(xv_lo_ready, b + 1)
            for i, (xi, w) in enumerate(((0, a_w_lo[2]), (1, a_w_hi[2]), (0, a_w_hi[2]))):
                last = nc.tensor.matmul(ps_v[:, :], xv_half[:, xi, kb * P:(kb + 1) * P],
                                        w[:, half * 512:(half + 1) * 512], start=(i == 0), stop=(i == 2))
            last.then_inc(v_done, 1)

        def a_qk(b, j):
            pe = nc.tensor
            g = 8 * b + j
            if not (isinstance(b, int) and b == 0 and j < 2):
                pe.wait_ge(qk_lo_ready, 2 * (g - 1))
            if j == 0:
                pe.wait_ge(xq_copied, 16 * (b + 1))
            x = xq_half[:, bass.ds(b % 2, 1)].rearrange("p o a s -> p (o a) s")
            for k in range(2):
                for i, (w, xi) in enumerate(((a_w_lo, 0), (a_w_hi, 1), (a_w_hi, 0))):
                    last = nc.tensor.matmul(ps_qk[j % 2][:, k * S:(k + 1) * S], w[k][:, j * P:(j + 1) * P], x[:, xi, :],
                                            start=(i == 0), stop=(i == 2))
            last.then_inc(qk_done, 1)

        def a_scores(b, j):
            pe = nc.tensor
            g = 8 * b + j
            pe.wait_ge(qk_lo_ready, 2 * (g + 1))
            if not (isinstance(b, int) and b == 0 and j < 2):
                pe.wait_ge(e_ready, 2 * (g - 1))
            for h in range(2):
                rows = slice(h * P0, (h + 1) * P0)
                for kb in range(TB):
                    dst, keys = ps_s[2 * (j % 2) + h][:, kb * S:(kb + 1) * S], slice(kb * P, (kb + 1) * P)
                    for i, (k, q) in enumerate(((k_hi, q_lo), (k_lo, q_hi), (k_hi, q_hi))):
                        last = nc.tensor.matmul(dst, k[j % 2][rows, keys], q[j % 2][rows, :],
                                                start=(i == 0), stop=(i == 2))
                last.then_inc(s_done, 1)

        def a_pv(b, j):
            pe = nc.tensor
            g = 8 * b + j
            pe.wait_ge(vn_ready, g + 1)
            pe.wait_ge(e_ready, 2 * (g + 1))
            if not (isinstance(b, int) and b == 0 and j < 1):
                pe.wait_ge(c_ready, g)
            for kb in range(TB):
                for h in range(2):
                    lo = h * P0
                    last = nc.tensor.matmul(ps_c[lo:lo + P0, (j % 2) * S:(j % 2 + 1) * S],
                                            vn_sb[j % 2][:, kb, h, :], e_sb[j % 2][:, h, kb, :],
                                            start=(kb == 0), stop=(kb == TB - 1))
            last.then_inc(c_done, 1)

        def a_out(b):
            pe = nc.tensor
            pe.wait_ge(c_ready, 8 * (b + 1))
            pe.wait_ge(v_ready, min(4 * b + 6, 4 * NB) if isinstance(b, int) else 4 * b + 6)
            if not (isinstance(b, int) and b < 2):
                pe.wait_ge(rwT_ready, b - 1)
            for tb in range(TB):
                for j in range(NJ):
                    last = nc.tensor.matmul(ps_v[:, tb * P:(tb + 1) * P], ctxT[:, j, tb * P:(tb + 1) * P],
                                            lw[:, j, :], start=(j == 0), stop=(j == NJ - 1))
            last.then_inc(o_done, 1)

        def a_x1T(b):
            nc.tensor.wait_ge(x1_ready, TB * (b + 1))
            nc.tensor.wait_ge(v_ready, min(4 * b + 8, 4 * NB) if isinstance(b, int) else 4 * b + 8)
            nc.tensor.wait_ge(y_ready, b + 1)
            for tb in range(TB):
                last = nc.tensor.transpose(ps_v[:, tb * P:(tb + 1) * P], x1s[:, tb, :], ident[:, :])
            last.then_inc(x1T_done, 1)

        def a_logits(b):
            nc.tensor.wait_ge(x1T_ready, b + 1)
            for tb in range(TB):
                last = nc.tensor.matmul(ps_v[:, tb * E:(tb + 1) * E], x1Ts[:, tb * P:(tb + 1) * P],
                                        gate_w[:, :], start=True, stop=True)
            last.then_inc(logit_done, 1)

        def a_rwT(b, v_parts, logits):
            nc.tensor.wait_ge(rw_ready, 2 * (b + 1))
            nc.tensor.wait_ge(v_ready, v_parts)
            nc.tensor.wait_ge(r_exp_ready, logits)
            if not (isinstance(b, int) and b == 0):
                nc.tensor.wait_ge(rwT_ready, b)
            for tb in range(TB):
                last = nc.tensor.transpose(ps_v[:, tb * P:(tb + 1) * P],
                                           rw_st[:, tb].rearrange("p a e -> p (a e)"), ident[:, :])
            last.then_inc(rwT_done, 1)

        def pair(b, j):
            return (b - 1, j + NJ) if j < 0 else (b + 1, j - NJ) if j >= NJ else (b, j)

        def a_pe_batch(b, first, second, last):
            for j in range(NJ):
                if j > 0 or not first:
                    a_pv(*pair(b, j - 1))
                if j < 6 or not last:
                    a_qk(*pair(b, j + 2))
                if j < 7 or not last:
                    a_scores(*pair(b, j + 1))
                if j == 0 and not first:
                    a_out(b - 1)
                if j in (1, 2):
                    a_v_part(b, 1, j - 1)
                if j in (5, 6) and not last:
                    a_v_part(b + 1, 0, j - 5)
                if not first:
                    if j == 3:
                        a_x1T(b - 1)
                    if j == 4:
                        a_logits(b - 1)
                if not second:
                    if j == 7:
                        a_rwT(b - 2, 4 * b + (4 if last else 6), b)

        def a_qk_out(b, j):
            g = 8 * b + j
            nc.scalar.wait_ge(qk_done, g + 1)
            nc.scalar.activation(q_hi[j % 2][:, :], ps_qk[j % 2][:, 0:S], ACT.Identity, bias=qb8[:, j:j + 1],
                                 scale=1.0).then_inc(qk_ready, 1)
            nc.scalar.activation(k_hi[j % 2][:, :], ps_qk[j % 2][:, S:2 * S], ACT.Identity, bias=kb_[:, j:j + 1],
                                 scale=1.0).then_inc(qk_ready, 1)

        def a_c_out(b, j):
            nc.scalar.wait_ge(c_done, 8 * b + j + 1)
            nc.scalar.copy(ctxT[:, j, :], ps_c[:, (j % 2) * S:(j % 2 + 1) * S]).then_inc(c_ready, 1)

        def a_exp(b, j, h):
            nc.scalar.wait_ge(max_ready, 2 * (8 * b + j) + h + 1)
            for kb in range(TB):
                last = nc.scalar.activation(e_sb[j % 2][:, h, kb, :],
                                            ps_s[2 * (j % 2) + h][:, kb * S:(kb + 1) * S], ACT.Exp,
                                            bias=nmax[:, j, kb, h:h + 1], scale=1.0,
                                            accum_out=esum[:, j, kb, h:h + 1])
            last.then_inc(e_ready, 1)

        def a_x1T_out(b):
            nc.scalar.wait_ge(x1T_done, b + 1)
            if not (isinstance(b, int) and b == 0):
                nc.scalar.wait_ge(x1T_stored, 16 * b)
            nc.scalar.copy(x1Ts[:, :], ps_v[:, 0:S]).then_inc(x1T_ready, 1)

        def a_r_exp(b):
            nc.scalar.wait_ge(logit_done, b + 1)
            nc.scalar.activation(r_exp[:, :, :].rearrange("p t e -> p (t e)"), ps_v[:, 0:TB * E], ACT.Exp,
                                 scale=-1.0).then_inc(r_exp_ready, 1)

        def a_rwT_out(b):
            nc.scalar.wait_ge(rwT_done, b + 1)
            if not (isinstance(b, int) and b == 0):
                nc.scalar.wait_ge(rwT_stored, 16 * b)
            nc.scalar.copy(rwTs[:, :], ps_v[:, 0:S]).then_inc(rwT_ready, 1)

        def a_act_batch(b, first, second, last):
            for j in range(NJ):
                if j == 4 and not first:
                    a_x1T_out(b - 1)
                if j == 5 and not first:
                    a_r_exp(b - 1)
                if j > 0 or not first:
                    a_c_out(*pair(b, j - 1))
                if j < 6 or not last:
                    a_qk_out(*pair(b, j + 2))
                if j < 7 or not last:
                    a_exp(*pair(b, j + 1), 0)
                    a_exp(*pair(b, j + 1), 1)
                if j == 7 and not second:
                    a_rwT_out(b - 2)

        def a_max(b, j):
            for h in range(2):
                nc.vector.wait_ge(s_done, 2 * (8 * b + j) + h + 1)
                nc.vector.tensor_reduce(nmax[:, j, :, h],
                                        ps_s[2 * (j % 2) + h][:, :].rearrange("p (k q) -> p k q", k=TB),
                                        AX.X, ALU.max, negate=True).then_inc(max_ready, 1)

        def a_rec(b, j):
            nc.vector.wait_ge(e_ready, 2 * (8 * b + j + 1))
            nc.vector.reciprocal(erec[:, j], esum[:, j]).then_inc(rec_ready, 1)

        def a_qk_lo(b, j):
            v = nc.vector
            v.wait_ge(qk_ready, 2 * (8 * b + j + 1))
            v.scalar_tensor_tensor(q_lo[j % 2][:, :], ps_qk[j % 2][:, 0:S], qb8[:, j:j + 1],
                                   q_hi[j % 2][:, :].bitcast(FP32), ALU.add, ALU.subtract).then_inc(qk_lo_ready, 1)
            v.scalar_tensor_tensor(k_lo[j % 2][:, :], ps_qk[j % 2][:, S:2 * S], kb_[:, j:j + 1],
                                   k_hi[j % 2][:, :].bitcast(FP32), ALU.add, ALU.subtract).then_inc(qk_lo_ready, 1)

        def a_v_out(b, half, kb):
            nc.vector.wait_ge(v_done, 4 * b + 2 * half + kb + 1)
            if not (isinstance(b, int) and b == 0):
                nc.vector.wait_ge(vn_ready, 8 * b if half else 8 * b - 4)
            cols = slice(half * 512, (half + 1) * 512)
            nc.vector.tensor_tensor(v_sb[:, kb, cols], ps_v[:, :], vb[:, cols], ALU.add).then_inc(v_ready, 1)

        def a_y(b):
            nc.vector.wait_ge(o_done, b + 1)
            nc.vector.wait_ge(xrl_ready, b + 1)
            nc.vector.tensor_tensor(y_sb[:, 0:TB, :], ps_v[:, 0:S].rearrange("p (t d) -> p t d", t=TB),
                                    xrl[:, :, :], ALU.add).then_inc(y_ready, 1)

        def a_stats(b):
            nc.vector.wait_ge(y_ready, b + 1)
            for tb in range(TB):
                nc.vector.bn_stats(st6[:, tb, :], y_sb[:, tb, :]).then_inc(stats_ready, 1)
            nc.vector.wait_ge(stats_ready, TB * (b + 1))
            own_wait()
            for tb in range(TB):
                nc.vector.bn_aggr(mv[:, tb, :], st6[:, tb, :]).then_inc(mv_ready, 1)

        def a_norm(b):
            nc.vector.wait_ge(rstd_ready, b + 1)
            if not (isinstance(b, int) and b == 0):
                nc.vector.wait_ge(x1_stored, 16 * b)
            for tb in range(TB):
                nc.vector.tensor_scalar(x1s[:, tb, :], y_sb[:, tb, :], mv[:, tb, 0:1], rstd[:, tb:tb + 1],
                                        ALU.subtract, ALU.mult).then_inc(x1_ready, 1)

        ROUTE_STEPS = 20

        def router(b, n):
            n = [n]

            def step(ins):
                n[0] += 1
                ins.then_inc(rt, 1)
                nc.vector.wait_ge(rt, ROUTE_STEPS * b + n[0])

            return step

        def route_scores(b):
            step = router(b, 0)
            v = nc.vector
            v.wait_ge(r_exp_ready, b + 1)
            step(v.tensor_scalar(r_one[:], r_exp[:], 1.0, None, ALU.add))
            step(v.reciprocal(score[:], r_one[:]))
            step(v.tensor_tensor(choice[:], score[:], gate_b[:, :].unsqueeze(1).broadcast_to([P, TB, E]), ALU.add))

        def route_best_two(b):
            step = router(b, 3)
            v = nc.vector
            for tb in range(TB):
                for g in range(NG):
                    last = v.max(top[:, tb, g, :], choice[:, tb, g * GE:(g + 1) * GE])
            step(last)
            step(v.tensor_tensor(gsum[:], top[:, :, :, 0], top[:, :, :, 1], ALU.add))

        def route_groups(b):
            step = router(b, 5)
            v = nc.vector
            mine = gsum[:].unsqueeze(3).broadcast_to([P, TB, NG, NG])
            other = gsum[:].unsqueeze(2).broadcast_to([P, TB, NG, NG])
            v.tensor_tensor(g_gt[:], other, mine, ALU.is_gt)
            step(v.tensor_tensor(g_eq[:], other, mine, ALU.is_equal))
            step(v.tensor_tensor(g_tie[:], g_eq[:], tri[:].unsqueeze(1).broadcast_to([P, TB, NG, NG]), ALU.mult))
            step(v.tensor_tensor(g_cnt[:], g_gt[:], g_tie[:], ALU.add))
            step(v.tensor_reduce(rank[:], g_cnt[:], AX.X, ALU.add))
            step(v.tensor_scalar(gmask[:], rank[:], float(KEEP_GROUPS), None, ALU.is_lt))

        def route_best_eight(b):
            step = router(b, 10)
            v = nc.vector
            grouped = lambda a: a[:].rearrange("p t (g e) -> p (t g) e", g=NG)
            step(v.tensor_tensor(grouped(masked), grouped(choice),
                                 gmask[:].rearrange("p t g -> p (t g)").unsqueeze(2).broadcast_to([P, TB * NG, GE]),
                                 ALU.mult))
            step(v.tensor_scalar(masked0[:], masked[:], 0.0, None, ALU.add))
            own_wait()
            for tb in range(TB):
                last = v.max(top8[:, tb, :], masked0[:, tb, :])
            step(last)
            own_wait()
            for tb in range(TB):
                last = v.match_replace(marked[:, tb, :], top8[:, tb, :], masked0[:, tb, :], FAR)
            step(last)
            step(v.tensor_scalar(sel[:], marked[:], 0.5 * FAR, None, ALU.is_ge))

        def route_weights(b):
            step = router(b, 15)
            v = nc.vector
            step(v.tensor_tensor(wsel[:], score[:], sel[:], ALU.mult))
            step(v.tensor_reduce(wsum[:], wsel[:], AX.X, ALU.add))
            step(v.tensor_scalar(wsum2[:], wsum[:], 1e-20, None, ALU.add))
            step(v.reciprocal(wrec[:], wsum2[:]))
            step(v.tensor_scalar(wrec2[:], wrec[:], ROUTED_SCALE, None, ALU.mult))
            if not (isinstance(b, int) and b == 0):
                v.wait_ge(rwT_done, b)
            for tb in range(TB):
                last = v.tensor_scalar(rw[:, tb, :], wsel[:, tb, :], wrec2[:, tb:tb + 1], None, ALU.mult)
            last.then_inc(rw_full, 1)
            v.wait_ge(rw_full, b + 1)
            v.tensor_copy(rw_hi[:], rw[:]).then_inc(rw_split, 1)
            v.wait_ge(rw_split, b + 1)
            v.tensor_copy(rw_st[:, :, 0, :], rw_hi[:].bitcast(FP32)).then_inc(rw_ready, 1)
            v.tensor_tensor(rw_st[:, :, 1, :], rw[:], rw_hi[:].bitcast(FP32), ALU.subtract).then_inc(rw_ready, 1)

        rw_full = sem("rw_full")
        rw_split = sem("rw_split")

        def a_dve_batch(b, first, second, last):
            for j in range(NJ):
                if j in (2, 3):
                    a_v_out(b, 1, j - 2)
                if j in (6, 7) and not last:
                    a_v_out(b + 1, 0, j - 6)
                if j == 1 and not first:
                    a_y(b - 1)
                a_rec(b, j)
                if j < 7 or not last:
                    a_max(*pair(b, j + 1))
                if j < 6 or not last:
                    a_qk_lo(*pair(b, j + 2))
                if not first:
                    if j == 1:
                        a_stats(b - 1)
                    if j == 2:
                        a_norm(b - 1)
                    if j == 6:
                        route_scores(b - 1)
                    if j == 7:
                        route_best_two(b - 1)
                if not second:
                    if j == 0:
                        route_groups(b - 2)
                    if j == 3:
                        route_best_eight(b - 2)
                    if j == 4:
                        route_weights(b - 2)

        def a_vn(b, j):
            g = 8 * b + j
            p = nc.gpsimd
            p.wait_ge(v_ready, 4 * b + (2 if j < 4 else 4))
            p.wait_ge(rec_ready, g + 1)
            if not (isinstance(b, int) and b == 0 and j < 2):
                p.wait_ge(c_done, g - 1)
            p.tensor_tensor(vn_sb[j % 2][:], v_sb[:, :, j * P:(j + 1) * P].rearrange("p k (h d) -> p k h d", h=2),
                            erec[:, j].unsqueeze(3).broadcast_to([P, TB, 2, P0]), ALU.mult).then_inc(vn_ready, 1)

        def a_xrl(b):
            p = nc.gpsimd
            p.wait_ge(xr_loaded, 16 * (b + 1))
            if not (isinstance(b, int) and b == 0):
                p.wait_ge(y_ready, b)
            p.tensor_tensor(xrl[:], xr[:], lb[:].unsqueeze(1).broadcast_to([P, TB, D]), ALU.add).then_inc(xrl_ready, 1)

        def a_x_half(b):
            p = nc.gpsimd
            p.wait_ge(xv_loaded, 16 * (b + 1))
            if not (isinstance(b, int) and b == 0):
                p.wait_ge(v_done, 4 * b)
                p.wait_ge(xq_copied, 16 * b)
            p.tensor_tensor(xv_half[:, 0], xv[:], one[:, 0:1].broadcast_to([P, S]), ALU.mult).then_inc(xv_hi_ready, 1)
            p.wait_ge(xv_hi_ready, b + 1)
            p.tensor_tensor(xv_half[:, 1], xv[:], xv_half[:, 0].bitcast(FP32), ALU.subtract).then_inc(xv_lo_ready, 1)

        def a_rstd(b):
            p = nc.gpsimd
            p.wait_ge(mv_ready, TB * (b + 1))
            p.tensor_tensor(veps[:, 0:TB], mv[:, 0:TB, 1], eps[:, 0:TB], ALU.add).then_inc(veps_ready, 1)
            p.wait_ge(veps_ready, b + 1)
            p.tensor_tensor(rstd[:, 0:TB], veps[:, 0:TB], minus_half[:, 0:TB], ALU.pow).then_inc(rstd_ready, 1)

        def a_pool_batch(b, first, second, last):
            for j in range(NJ):
                a_vn(b, j)
                if not first:
                    if j == 1:
                        a_rstd(b - 1)
                if j == 2 and not last:
                    a_x_half(b + 1)
                if j == 4:
                    a_xrl(b)

        def a_store_x1(b):
            nc.sync.wait_ge(x1_ready, TB * (b + 1))
            nc.sync.dma_start(x1_d.rearrange("(n p) d -> p n d", p=P)[:, bass.ds(b * TB, TB), :],
                              x1s[:]).then_inc(x1_stored, 16)
            nc.sync.wait_ge(x1T_ready, b + 1)
            nc.sync.dma_start(x1T_d[:, bass.ds(b * S, S)], x1Ts[:]).then_inc(x1T_stored, 16)

        def a_store_rwT(b):
            nc.sync.wait_ge(rwT_ready, b + 1)
            nc.sync.dma_start(rwT_d[:, bass.ds(b * S, S)], rwTs[:].bitcast(FP32)).then_inc(rwT_stored, 16)

        def a_load_x(b):
            if not (isinstance(b, int) and b == 0):
                nc.sync.wait_ge(xv_lo_ready, b)
            nc.sync.dma_start(xv[:, :], t["xT"][:, bass.ds(b * S, S)]).then_inc(xv_loaded, 16)

        def a_copy_x(b):
            nc.sync.wait_ge(xv_lo_ready, b + 1)
            nc.sync.dma_start(xq_half[:, bass.ds(b % 2, 1)].rearrange("p o a s -> p (o a s)").bitcast(FP32),
                              xv_half[:].rearrange("p a s -> p (a s)").bitcast(FP32)).then_inc(xq_copied, 16)

        def a_sp_batch(b, first, second, last):
            if not last:
                a_load_x(b + 1)
            if not first:
                a_store_x1(b - 1)
            if not last:
                nc.sync.wait_ge(xrl_ready, b + 1)
                nc.sync.dma_start(xr[:], t["x"].rearrange("(n p) d -> p n d", p=P)[:, bass.ds((b + 1) * TB, TB), :]
                                  ).then_inc(xr_loaded, 16)
                a_copy_x(b + 1)
            if not second:
                a_store_rwT(b - 2)

        ps_g, ps_u, ps_r, ps_acc, ps_t = bank[0:2], bank[2:4], bank[4:6], bank[6], bank[7]

        w_hi_loaded = sem("w_hi_loaded")
        raw_loaded = [sem(f"raw_loaded{i}") for i in range(2)]
        lo_ready = sem("lo_ready")
        xf_loaded = sem("xf_loaded")
        rw_loaded = [sem(f"rw_loaded{i}") for i in range(2)]
        xres_loaded = sem("xres_loaded")
        x_hi_ready = sem("x_hi_ready")
        x_lo_ready = sem("x_lo_ready")
        g_done = sem("g_done")
        u_done = sem("u_done")
        r_done = sem("r_done")
        d_done = sem("d_done")
        sg_ready = sem("sg_ready")
        t_ready = sem("t_ready")
        hf_ready = sem("hf_ready")
        h_hi_ready = sem("h_hi_ready")
        h_lo_ready = sem("h_lo_ready")
        oT_ready = sem("oT_ready")
        ot_done = sem("ot_done")
        y2_ready = sem("y2_ready")
        stats2_ready = sem("stats2_ready")
        mv2_ready = sem("mv2_ready")
        veps2_ready = sem("veps2_ready")
        rstd2_ready = sem("rstd2_ready")
        x2_ready = sem("x2_ready")
        x2T_done = sem("x2T_done")
        x2T_ready = sem("x2T_ready")
        x2_stored = sem("x2_stored")
        x2T_stored = sem("x2T_stored")
        GATE, UP, DOWN = range(3)

        def past(n, c, lag):
            return not (isinstance(n, int) and n * NC + c < lag)

        def three(out, c, which, hi, lo, start, stop):
            nc.tensor.matmul(out, w_lo[:, c, which, :], hi, start=start, stop=False)
            nc.tensor.matmul(out, w_hi[:, c, which, :], lo, start=False, stop=False)
            return nc.tensor.matmul(out, w_hi[:, c, which, :], hi, start=False, stop=stop)

        def b_up(n, c, par):
            pe = nc.tensor
            s = n * NC + c
            q = n * NCR + c
            if c == 0:
                pe.wait_ge(x_hi_ready, n + 1)
                pe.wait_ge(x_lo_ready, n + 1)
            if isinstance(n, int) and n == 0:
                pe.wait_ge(lo_ready, c + 1)
            if past(n, c, 2):
                pe.wait_ge(sg_ready, s - 1)
            three(ps_g[c % 2][:, :], c, GATE, x_hi[par][:, :], x_lo[par][:, :], True, True).then_inc(g_done, 1)
            if past(n, c, 2):
                pe.wait_ge(t_ready, s - 1)
            three(ps_u[c % 2][:, :], c, UP, x_hi[par][:, :], x_lo[par][:, :], True, True).then_inc(u_done, 1)
            if c < NCR:
                if c == 0:
                    pe.wait_ge(rw_loaded[par], 8 * (n + 2 - par))
                if past(n, c, 2):
                    pe.wait_ge(hf_ready, q - 1)
                nc.tensor.matmul(ps_r[c % 2][:, :], select[:, c, :], rw_in[par][:, :],
                                 start=True, stop=True).then_inc(r_done, 1)

        def b_down(n, c):
            pe = nc.tensor
            s = n * NC + c
            pe.wait_ge(h_hi_ready, s + 1)
            pe.wait_ge(h_lo_ready, s + 1)
            if c == 0 and past(n, c, 1):
                pe.wait_ge(oT_ready, n)
            three(ps_acc[:, :], c, DOWN, h_hi[c % 2][:, :], h_lo[c % 2][:, :], c == 0,
                  c == NC - 1).then_inc(d_done, 1)

        def b_oT(n):
            nc.tensor.wait_ge(oT_ready, n + 1)
            if past(n, 0, 1):
                nc.tensor.wait_ge(x2T_ready, n)
            for k in range(SUB):
                last = nc.tensor.transpose(ps_t[:, k * P:(k + 1) * P], oT[:, k * P:(k + 1) * P], ident[:, :])
            last.then_inc(ot_done, 1)

        def b_x2T(n):
            nc.tensor.wait_ge(x2_ready, SUB * (n + 1))
            nc.tensor.wait_ge(y2_ready, n + 1)
            for k in range(SUB):
                last = nc.tensor.transpose(ps_t[:, k * P:(k + 1) * P], x2s[:, k, :], ident[:, :])
            last.then_inc(x2T_done, 1)

        def b_pe_tile(n, par, first):
            for c in range(NC):
                b_up(n, c, par)
                if c >= 2:
                    b_down(n, c - 2)
                elif not first:
                    b_down(n - 1, NC + c - 2)
                if not first:
                    if c == 2:
                        b_oT(n - 1)
                    if c == 12:
                        b_x2T(n - 1)

        def b_silu(n, c):
            s = n * NC + c
            nc.scalar.wait_ge(g_done, s + 1)
            if past(n, c, 2):
                nc.scalar.wait_ge(t_ready, s - 1)
            nc.scalar.activation(sg[c % 2][:, :], ps_g[c % 2][:, :], ACT.Silu).then_inc(sg_ready, 1)

        def b_h_hi(n, c):
            s = n * NC + c
            if c < NCR:
                nc.scalar.wait_ge(hf_ready, n * NCR + c + 1)
            else:
                nc.scalar.wait_ge(t_ready, s + 1)
            if past(n, c, 2):
                nc.scalar.wait_ge(d_done, s - 1)
            nc.scalar.copy(h_hi[c % 2][:, :], hf[c % 2][:, :]).then_inc(h_hi_ready, 1)

        def b_oT_out(n):
            nc.scalar.wait_ge(d_done, NC * (n + 1))
            if past(n, 0, 1):
                nc.scalar.wait_ge(ot_done, n)
            nc.scalar.copy(oT[:, :], ps_acc[:, :]).then_inc(oT_ready, 1)

        def b_x2T_out(n):
            nc.scalar.wait_ge(x2T_done, n + 1)
            if past(n, 0, 1):
                nc.scalar.wait_ge(x2T_stored, 16 * n)
            nc.scalar.copy(x2Ts[:, :], ps_t[:, :]).then_inc(x2T_ready, 1)

        def b_x_hi(n, par):
            nc.scalar.wait_ge(xf_loaded, 16 * (n + 1))
            nc.scalar.copy(x_hi[par][:, :], xf[:, :]).then_inc(x_hi_ready, 1)

        def b_act_tile(n, par, first, last):
            for c in range(NC):
                b_silu(n, c)
                if c >= 1:
                    b_h_hi(n, c - 1)
                elif not first:
                    b_h_hi(n - 1, NC - 1)
                if not first:
                    if c == 2:
                        b_oT_out(n - 1)
                    if c == 12:
                        b_x2T_out(n - 1)
                if c == 20 and not last:
                    b_x_hi(n + 1, 1 - par)

        def b_lo(c):
            nc.vector.wait_ge(raw_loaded[c % 2], 16 * (c // 2 + 1))
            nc.vector.tensor_tensor(w_lo[:, c], w_raw[:, c % 2], w_hi[:, c].bitcast(FP32),
                                    ALU.subtract).then_inc(lo_ready, 1)

        def b_h(n, c):
            v = nc.vector
            s = n * NC + c
            v.wait_ge(sg_ready, s + 1)
            v.wait_ge(u_done, s + 1)
            if past(n, c, 2):
                v.wait_ge(h_lo_ready, s - 1)
            v.tensor_tensor(hf[c % 2][:, :], sg[c % 2][:, :], ps_u[c % 2][:, :], ALU.mult).then_inc(t_ready, 1)
            if c < NCR:
                v.wait_ge(t_ready, s + 1)
                v.wait_ge(r_done, n * NCR + c + 1)
                v.tensor_tensor(hf[c % 2][:, :], hf[c % 2][:, :], ps_r[c % 2][:, :],
                                ALU.mult).then_inc(hf_ready, 1)

        def b_y(n):
            v = nc.vector
            v.wait_ge(ot_done, n + 1)
            v.wait_ge(xres_loaded, 16 * (n + 1))
            v.tensor_tensor(y2[:], ps_t[:, :].rearrange("p (k d) -> p k d", k=SUB), xres[:],
                            ALU.add).then_inc(y2_ready, 1)

        def b_stats(n):
            v = nc.vector
            v.wait_ge(y2_ready, n + 1)
            for k in range(SUB):
                v.bn_stats(st6[:, k, :], y2[:, k, :]).then_inc(stats2_ready, 1)

        def b_mv(n):
            v = nc.vector
            v.wait_ge(stats2_ready, SUB * (n + 1))
            own_wait()
            for k in range(SUB):
                v.bn_aggr(mv[:, k, :], st6[:, k, :]).then_inc(mv2_ready, 1)

        def b_norm(n, ks):
            v = nc.vector
            v.wait_ge(rstd2_ready, n + 1)
            if past(n, 0, 1):
                v.wait_ge(x2_stored, 16 * n)
            for k in ks:
                v.tensor_scalar(x2s[:, k, :], y2[:, k, :], mv[:, k, 0:1], rstd[:, k:k + 1],
                                ALU.subtract, ALU.mult).then_inc(x2_ready, 1)

        def b_dve_tile(n, first):
            for c in range(NC):
                if first and c + 2 < NC:
                    b_lo(c + 2)
                b_h(n, c)
                if not first:
                    if c == 3:
                        b_y(n - 1)
                    if c == 5:
                        b_stats(n - 1)
                    if c == 6:
                        b_mv(n - 1)
                    if c == 8:
                        b_norm(n - 1, (0, 1))
                    if c == 9:
                        b_norm(n - 1, (2, 3))

        def b_h_lo(n, c):
            p = nc.gpsimd
            s = n * NC + c
            p.wait_ge(h_hi_ready, s + 1)
            if past(n, c, 2):
                p.wait_ge(d_done, s - 1)
            p.tensor_tensor(h_lo[c % 2][:, :], hf[c % 2][:, :], h_hi[c % 2][:, :].bitcast(FP32),
                            ALU.subtract).then_inc(h_lo_ready, 1)

        def b_x_lo(n, par):
            p = nc.gpsimd
            p.wait_ge(x_hi_ready, n + 1)
            p.tensor_tensor(x_lo[par][:, :], xf[:, :], x_hi[par][:, :].bitcast(FP32),
                            ALU.subtract).then_inc(x_lo_ready, 1)

        def b_rstd(n):
            p = nc.gpsimd
            p.wait_ge(mv2_ready, SUB * (n + 1))
            p.tensor_tensor(veps[:, :], mv[:, :, 1], eps[:, :], ALU.add).then_inc(veps2_ready, 1)
            p.wait_ge(veps2_ready, n + 1)
            p.tensor_tensor(rstd[:, :], veps[:, :], minus_half[:, :], ALU.pow).then_inc(rstd2_ready, 1)

        def b_pool_tile(n, par, first, last):
            for c in range(NC):
                b_h_lo(n, c)
                if c == 6 and not first:
                    b_rstd(n - 1)
                if c == 21 and not last:
                    b_x_lo(n + 1, 1 - par)

        def b_load(n, par):
            sp = nc.sync
            if past(n, 0, 1):
                sp.wait_ge(x_lo_ready, n)
            sp.dma_start(xf[:, :], x1T_d[:, bass.ds(n * TILE, TILE)]).then_inc(xf_loaded, 16)
            if not (isinstance(n, int) and n < 2):
                sp.wait_ge(r_done, NCR * (n - 1))
            sp.dma_start(rw_in[par][:, :].bitcast(FP32), rwT_d[:, bass.ds(n * TILE, TILE)]).then_inc(rw_loaded[par], 16)

        def b_load_res(n):
            sp = nc.sync
            if past(n, 0, 1):
                sp.wait_ge(y2_ready, n)
            sp.dma_start(xres[:], x1_d.rearrange("(n p) d -> p n d", p=P)[:, bass.ds(n * SUB, SUB), :]
                         ).then_inc(xres_loaded, 16)

        def b_store(n):
            sp = nc.sync
            sp.wait_ge(x2_ready, SUB * (n + 1))
            sp.dma_start(x2_d.rearrange("(n p) d -> p n d", p=P)[:, bass.ds(n * SUB, SUB), :],
                         x2s[:]).then_inc(x2_stored, 16)
            sp.wait_ge(x2T_ready, n + 1)
            sp.dma_start(x2T_d[:, bass.ds(n * TILE, TILE)], x2Ts[:, :]).then_inc(x2T_stored, 16)

        def b_raw(c):
            if c >= 2:
                nc.sync.wait_ge(lo_ready, c - 1)
            nc.sync.dma_start(w_raw[:, c % 2], t["w_all"][:, c * 3 * P:(c + 1) * 3 * P]
                              .rearrange("p (a m) -> p a m", a=3)).then_inc(raw_loaded[c % 2], 16)

        def b_sp():
            sp = nc.sync
            for c in range(2, NC):
                b_raw(c)
                if c == 8:
                    sp.wait_ge(x1T_stored, 16 * NB)
                    sp.wait_ge(x1_stored, 16 * NB)
                    sp.wait_ge(rwT_stored, 16 * NB)
                    b_load(1, 1)
            with sp.Fori(0, NTILE // 2 - 1) as k:
                n = k * 2 + 1
                b_load(n + 1, 0)
                b_load_res(n)
                b_store(n - 1)
                b_load(n + 2, 1)
                b_load_res(n + 1)
                b_store(n)
            b_load_res(NTILE - 1)
            b_store(NTILE - 2)

        ps_m, ps_x, ps_pv, ps_p, ps_tr, ps_tail = bank[0:2], bank[2:4], bank[4], bank[5], bank[6], bank[7]
        NPAIR = NB // 2

        c_loaded = sem("c_loaded")
        c_prep = sem("c_prep")
        pad_ready = sem("pad_ready")
        x_kv_loaded = sem("x_kv_loaded")
        x_q_loaded = sem("x_q_loaded")
        p_done = sem("p_done")
        p_ready = sem("p_ready")
        hi_ready = sem("hi_ready")
        split_ready = sem("split_ready")
        alone_zeroed = sem("alone_zeroed")
        k_alone_ready = [sem(f"k_alone_ready{j}") for j in range(4)]
        m_done = sem("m_done")
        mx_ready = sem("mx_ready")
        mx_hi_ready = sem("mx_hi_ready")
        pad_set = sem("pad_set")
        t_done = sem("t_done")
        q_x_ready = sem("q_x_ready")
        x_done = sem("x_done")
        p_exp_ready = sem("p_exp_ready")
        pv_done = sem("pv_done")
        aT_ready = sem("aT_ready")
        atr_done = sem("atr_done")
        den_ready = sem("den_ready")
        an_ready = sem("an_ready")
        anT_done = sem("anT_done")
        anT_ready = sem("anT_ready")
        wo_done = sem("wo_done")
        xr3_loaded = sem("xr3_loaded")
        xr3b_ready = sem("xr3b_ready")
        y3_ready = sem("y3_ready")
        x3_ready = sem("x3_ready")
        x3b_ready = sem("x3b_ready")
        x3T_done = sem("x3T_done")
        x3T_ready = sem("x3T_ready")
        cb_done = sem("cb_done")
        z0_ready = sem("z0_ready")
        z1_ready = sem("z1_ready")
        res_ready = sem("res_ready")
        ln_st_ready = [sem(f"ln_st_ready{i}") for i in range(2)]
        ln_mv_ready = [sem(f"ln_mv_ready{i}") for i in range(2)]
        ln_ve_ready = [sem(f"ln_ve_ready{i}") for i in range(2)]
        ln_rs_ready = [sem(f"ln_rs_ready{i}") for i in range(2)]
        out_stored = sem("out_stored")

        def whole(b):
            return isinstance(b, int)

        USES = [{(0, 0): ("vt", 0, 0), (0, 2): ("k", 0, 1), (1, 0): ("k", 1, 1), (1, 2): ("k", 2, 1),
                 (2, 0): ("k", 3, 1), (2, 2): ("vt", 1, 0), (3, 0): ("vt", 2, 0), (3, 2): ("vt", 3, 0)},
                {(0, 0): ("v", 0, 1), (0, 2): ("q", 0, 2), (1, 0): ("v", 1, 1), (1, 2): ("q", 1, 2),
                 (2, 0): ("v", 2, 1), (2, 2): ("q", 2, 2), (3, 0): ("v", 3, 1), (3, 2): ("q", 3, 2)}]
        START = [("q", i, 1) for i in range(4)] + [("k", i, 1) for i in range(4)]

        def wanted(p, what, ahead):
            return not whole(p) or 0 <= p + ahead < NPAIR

        def use(p, u, k):
            if not whole(p):
                return 16 * (p + 1) + 8 * u + k
            n = 0
            for pp in range(-1, p + 1):
                for uu in range(2):
                    uses = START if (pp, uu) == (-1, 0) else list(USES[uu].values())
                    if (pp, uu) == (p, u):
                        return n + sum(wanted(pp, w, a) for w, _, a in uses[:k])
                    n += sum(wanted(pp, w, a) for w, _, a in uses)

        def start_bank(n):
            return (ps_p, ps_pv)[n % 2]

        def c_project(p, what, part, n, ahead, start=False):
            pe = nc.tensor
            to = start_bank(n) if start else ps_p
            if not start:
                pe.wait_ge(p_ready, n)
            elif n > 1:
                pe.wait_ge(p_ready, n - 1)
            src = x_q if what == "q" else x_kv
            if what == "q":
                pe.wait_ge(x_q_loaded, 16 * (p + ahead + 1))
            else:
                pe.wait_ge(x_kv_loaded, 16 * (p + ahead + 1))
            w = c_w[2] if what == "v" else c_wr["qk".index(what)]
            xs = src[:, :].rearrange("p (a g i) -> p a g i", a=8, g=GRP)
            for i in range(4):
                for g in range(GRP):
                    last = nc.tensor.matmul(to[W32 * g:W32 * (g + 1), i * P:(i + 1) * P], w[:, 4 * part + i, :],
                                            xs[:, :, g, :], start=True, stop=True, skip_group_check=True)
            last.then_inc(p_done, 1)

        def c_vt(p, part, n):
            nc.tensor.wait_ge(p_ready, n)
            for k in range(4):
                src = v_st[:, 2 * part + k // 2].rearrange("p c i -> p (c i)")
                last = nc.tensor.transpose(ps_p[:, k * P:(k + 1) * P], src[:, (k % 2) * P:(k % 2 + 1) * P],
                                           ident[:, :])
            last.then_inc(p_done, 1)

        def c_m(b, u, j, g):
            pe = nc.tensor
            n = 16 * b + 4 * j + g
            if g == 0:
                pe.wait_ge(split_ready, 2 * (4 * b + j + 1))
                pe.wait_ge(k_alone_ready[j], 16 * GRP * (b + 1))
            if not (whole(b) and n < 2):
                pe.wait_ge(mx_ready, n - 1)
            for qb in range(TB):
                last = nc.tensor.matmul(ps_m[g % 2][:, qb * S:(qb + 1) * S],
                                        q_m[u][:, j, qb * P:(qb + 1) * P], k_alone[u][:, j, g, :],
                                        start=True, stop=True)
            last.then_inc(m_done, 1)

        def c_t(b, j):
            pe = nc.tensor
            pe.wait_ge(pad_set, 2 * (4 * b + j + 1))
            if not (whole(b) and 4 * b + j == 0):
                pe.wait_ge(q_x_ready, 4 * b + j)
            for qb in range(TB):
                last = nc.tensor.transpose(ps_tr[:, qb * P:(qb + 1) * P],
                                           mx_pad[:, qb].rearrange("p g w -> p (g w)"), ident[:, :])
            last.then_inc(t_done, 1)

        def c_x(b, u, j, g):
            pe = nc.tensor
            n = 16 * b + 4 * j + g
            if g == 0:
                pe.wait_ge(q_x_ready, 4 * b + j + 1)
            if not (whole(b) and n < 2):
                pe.wait_ge(p_exp_ready, n - 1)
            for kb in range(TB):
                last = nc.tensor.matmul(ps_x[g % 2][:, kb * S:(kb + 1) * S],
                                        k_alone[u][:, j, g, kb * P:(kb + 1) * P], q_x[u][:, j, :],
                                        start=True, stop=True)
            last.then_inc(x_done, 1)

        def c_pv(b, u, p, j):
            pe = nc.tensor
            pe.wait_ge(p_exp_ready, 16 * b + 4 * j + 4)
            pe.wait_ge(p_ready, use(p, 0, (6 if j >= 2 else 1) if u == 0 else (8 if j >= 2 else 7)))
            if not (whole(b) and 4 * b + j == 0):
                pe.wait_ge(aT_ready, 4 * b + j)
            for kb in range(TB):
                for g in range(GRP):
                    lo = W32 * g
                    last = nc.tensor.matmul(ps_pv[lo:lo + W32, 0:S], vt[u][:, j, kb, lo:lo + W32],
                                            pt[j % 2][:, g, kb, :], start=(kb == 0), stop=(kb == TB - 1))
            last.then_inc(pv_done, 1)

        def c_atr(t, u, tb):
            pe = nc.tensor
            if tb == 0:
                pe.wait_ge(aT_ready, 4 * t + 4)
                if not (whole(t) and t == 0):
                    pe.wait_ge(z0_ready, t)
            else:
                pe.wait_ge(an_ready, 2 * t + 1)
            for j in range(4):
                last = nc.tensor.transpose(ps_tail[:, j * P:(j + 1) * P], aT[u][:, j, tb * P:(tb + 1) * P],
                                           ident[:, :])
            last.then_inc(atr_done, 1)

        def c_anT(t):
            nc.tensor.wait_ge(an_ready, 2 * t + 2)
            for tb in range(TB):
                last = nc.tensor.transpose(ps_tail[:, tb * P:(tb + 1) * P], an[:, tb, :], ident[:, :])
            last.then_inc(anT_done, 1)

        def c_wo_mm(t):
            nc.tensor.wait_ge(anT_ready, t + 1)
            for tb in range(TB):
                last = nc.tensor.matmul(ps_tail[:, tb * P:(tb + 1) * P], anT[:, tb * P:(tb + 1) * P], c_wo[:, :],
                                        start=True, stop=True)
            last.then_inc(wo_done, 1)

        def c_x3T(t):
            nc.tensor.wait_ge(x3_ready, 2 * t + 2)
            for tb in range(TB):
                last = nc.tensor.transpose(ps_tail[:, tb * P:(tb + 1) * P], x3s[:, tb, :], ident[:, :])
            last.then_inc(x3T_done, 1)

        def c_linear(t):
            nc.tensor.wait_ge(x3T_ready, t + 1)
            for tb in range(TB):
                last = nc.tensor.matmul(ps_tail[:, tb * P:(tb + 1) * P], x3T[:, tb * P:(tb + 1) * P], c_cb[:, :],
                                        start=True, stop=True)
            last.then_inc(cb_done, 1)

        def has(b):
            return not whole(b) or 0 <= b < NB

        def c_pe(b, u, p):
            for j in range(4):
                for g in range(GRP):
                    if has(b + 1):
                        c_m(b + 1, 1 - u, j, g)
                    if has(b):
                        c_x(b, u, j, g)
                    if (j, g) in USES[u]:
                        what, part, ahead = USES[u][j, g]
                        n = use(p, u, list(USES[u]).index((j, g)))
                        if wanted(p, what, ahead):
                            if what == "vt":
                                c_vt(p, part, n)
                            else:
                                c_project(p, what, part, n, ahead)
                    if g == 1:
                        if j == 0 and has(b):
                            c_t(b, 3)
                        if j > 0 and has(b + 1):
                            c_t(b + 1, j - 1)
                    if g == 2:
                        if j == 0 and has(b - 1):
                            c_pv(b - 1, 1 - u, p if u else p - 1, 3)
                        if j > 0 and has(b):
                            c_pv(b, u, p, j - 1)
                    if has(b - 1):
                        if (j, g) == (1, 0):
                            c_atr(b - 1, 1 - u, 0)
                        if (j, g) == (1, 2):
                            c_atr(b - 1, 1 - u, 1)
                        if (j, g) == (2, 0):
                            c_anT(b - 1)
                        if (j, g) == (2, 2):
                            c_wo_mm(b - 1)
                        if (j, g) == (3, 3):
                            c_x3T(b - 1)
                    if (j, g) == (0, 1) and has(b - 2):
                        c_linear(b - 2)

        def c_project_out(p, u, what, part, n, ahead, start=False):
            act = nc.scalar
            act.wait_ge(p_done, n + 1)
            k = "qkv".index(what)
            source = start_bank(n) if start else ps_p
            for i in range(4):
                c = 4 * part + i
                if what == "v":
                    dst = v_st[:, :, c, :]
                else:
                    par = (p + ahead) % 2
                    dst = qk_st[:, bass.ds(par, 1), :, k, c, :].rearrange("p o a i -> p (o a) i")
                last = act.activation(dst, source[:, i * P:(i + 1) * P].rearrange("p (a i) -> p a i", a=8),
                                      ACT.Identity, bias=c_br[:, k, c:c + 1], scale=1.0)
            last.then_inc(p_ready, 1)

        def c_vt_out(b, p, part, n):
            act = nc.scalar
            act.wait_ge(p_done, n + 1)
            if part >= 2 and not (whole(b) and b == 0):
                act.wait_ge(pv_done, 4 * b)
            act.copy(vt[part // 2][:, 2 * (part % 2):2 * (part % 2) + 2].rearrange("p j k m -> p (j k m)"),
                     ps_p[:, :]).then_inc(p_ready, 1)

        def c_exp(b, j, g):
            act = nc.scalar
            act.wait_ge(x_done, 16 * b + 4 * j + g + 1)
            if g == 0 and not (whole(b) and 4 * b + j < 2):
                act.wait_ge(pv_done, 4 * b + j - 1)
            act.activation(pt[j % 2][:, g].rearrange("p k q -> p (k q)"), ps_x[g % 2][:, :], ACT.Exp,
                           scale=float(D1) ** -0.5).then_inc(p_exp_ready, 1)

        def c_aT_out(b, u, j):
            nc.scalar.wait_ge(pv_done, 4 * b + j + 1)
            nc.scalar.copy(aT[u][:, j, :].rearrange("p (i c) -> p c i", c=CH),
                           ps_pv[:, 0:S].rearrange("p (c i) -> p c i", c=CH)).then_inc(aT_ready, 1)

        def c_anT_out(t):
            nc.scalar.wait_ge(anT_done, t + 1)
            nc.scalar.copy(anT[:, :], ps_tail[:, 0:S]).then_inc(anT_ready, 1)

        def c_x3T_out(t):
            nc.scalar.wait_ge(x3T_done, t + 1)
            nc.scalar.copy(x3T[:, :], ps_tail[:, 0:S]).then_inc(x3T_ready, 1)

        def c_act(b, u, p):
            for j in range(4):
                for g in range(GRP):
                    if (j, g) == (0, 0) and has(b - 2):
                        c_x3T_out(b - 2)
                    if (j, g) == (2, 1) and has(b - 1):
                        c_anT_out(b - 1)
                    if has(b):
                        c_exp(b, j, g)
                    if (j, g) in USES[u]:
                        what, part, ahead = USES[u][j, g]
                        n = use(p, u, list(USES[u]).index((j, g)))
                        if wanted(p, what, ahead):
                            if what == "vt":
                                c_vt_out(b, p, part, n)
                            else:
                                c_project_out(p, u, what, part, n, ahead)
                    if g == 3:
                        if j == 0 and has(b - 1):
                            c_aT_out(b - 1, 1 - u, 3)
                        if j > 0 and has(b):
                            c_aT_out(b, u, j - 1)

        def c_split(b, u, j):
            v = nc.vector
            n = 4 * b + j
            v.wait_ge(hi_ready, n + 1)
            if not (whole(b) and b < 2):
                v.wait_ge(x_done, 16 * (b - 2) + 4 * j + 4)
                v.wait_ge(k_alone_ready[j], 16 * GRP * (b - 1))
            par = (b // 2) % 2
            for k, dst in ((0, q_m), (1, k_m)):
                src = qk_st[:, bass.ds(par, 1), 4 * u + j, k].rearrange("p o c i -> p (o c i)")
                v.scalar_tensor_tensor(dst[u][:, j, :], qk_hi[j % 2][:, k, :].bitcast(FP32), c_low[:, k:k + 1],
                                       src, ALU.mult, ALU.add).then_inc(split_ready, 1)

        def c_max(b, j, g):
            v = nc.vector
            v.wait_ge(m_done, 16 * b + 4 * j + g + 1)
            v.tensor_reduce(mx[j % 2][:, :, g], ps_m[g % 2][:, :].rearrange("p (t k) -> p t k", t=TB), AX.X,
                            ALU.max).then_inc(mx_ready, 1)

        def c_pad(b, j):
            v = nc.vector
            n = 4 * b + j
            v.wait_ge(mx_ready, 4 * (n + 1))
            v.tensor_copy(mx_hi[:], mx[j % 2][:]).then_inc(mx_hi_ready, 1)
            v.wait_ge(mx_hi_ready, n + 1)
            if not (whole(b) and n == 0):
                v.wait_ge(t_done, n)
            v.tensor_copy(mx_pad[:, :, :, 0:19:18], mx_hi[:].bitcast(FP32).unsqueeze(3)
                          .broadcast_to([P, TB, GRP, 2])).then_inc(pad_set, 1)
            v.tensor_tensor(mx_pad[:, :, :, 9], mx[j % 2][:], mx_hi[:].bitcast(FP32),
                            ALU.subtract).then_inc(pad_set, 1)

        def c_q_x(b, u, j):
            v = nc.vector
            v.wait_ge(t_done, 4 * b + j + 1)
            v.tensor_tensor(q_x[u][:, j, :], ps_tr[:, 0:S], q_m[u][:, j, :].bitcast(FP32),
                            ALU.add).then_inc(q_x_ready, 1)

        def c_an(t, tb):
            v = nc.vector
            v.wait_ge(atr_done, 2 * t + tb + 1)
            heads = ps_tail[:, :].rearrange("p (h w) -> p h w", w=W32)
            v.reciprocal(den[:, tb, :], heads[:, :, 0]).then_inc(den_ready, 1)
            v.wait_ge(den_ready, 2 * t + tb + 1)
            if not (whole(t) and t == 0):
                v.wait_ge(anT_done, t)
            v.tensor_tensor(an[:, tb, :].rearrange("p (h d) -> p h d", d=D1), heads[:, :, 1:1 + D1],
                            den[:, tb, :].unsqueeze(2).broadcast_to([P, H1, D1]), ALU.mult).then_inc(an_ready, 1)

        def c_stats(i, t, y, ready):
            v = nc.vector
            v.wait_ge(ready, t + 1)
            for tb in range(TB):
                v.bn_stats(ln_st[i][:, tb, :], y[:, tb, :]).then_inc(ln_st_ready[i], 1)
            v.wait_ge(ln_st_ready[i], TB * (t + 1))
            own_wait()
            for tb in range(TB):
                v.bn_aggr(ln_mv[i][:, tb, :], ln_st[i][:, tb, :]).then_inc(ln_mv_ready[i], 1)

        def c_norm(i, t, y, dst, done):
            v = nc.vector
            v.wait_ge(ln_rs_ready[i], t + 1)
            for tb in range(TB):
                v.tensor_scalar(dst[:, tb, :], y[:, tb, :], ln_mv[i][:, tb, 0:1], ln_rs[i][:, tb:tb + 1],
                                ALU.subtract, ALU.mult).then_inc(done, 1)

        def c_y3(t):
            v = nc.vector
            v.wait_ge(wo_done, t + 1)
            v.wait_ge(xr3b_ready, t + 1)
            v.tensor_tensor(y3[:], ps_tail[:, 0:S].rearrange("p (t d) -> p t d", t=TB), xr3b[:],
                            ALU.add).then_inc(y3_ready, 1)

        def c_z(t):
            v = nc.vector
            v.wait_ge(cb_done, t + 1)
            v.tensor_tensor(z0[:], ps_tail[:, 0:S].rearrange("p (t d) -> p t d", t=TB),
                            c_scale[:].unsqueeze(1).broadcast_to([P, TB, D]), ALU.mult).then_inc(z0_ready, 1)
            v.wait_ge(z0_ready, t + 1)
            v.wait_ge(x3b_ready, t + 1)
            v.tensor_tensor(z1[:], z0[:], x3b[:], ALU.add).then_inc(z1_ready, 1)

        def c_dve(b, u, p):
            for j in range(4):
                for g in range(GRP):
                    if has(b + 1):
                        c_max(b + 1, j, g)
                    if g == 1:
                        if j == 0 and has(b):
                            c_q_x(b, u, 3)
                        if j > 0 and has(b + 1):
                            c_q_x(b + 1, 1 - u, j - 1)
                    if g == 0:
                        if j < 3 and has(b + 1):
                            c_split(b + 1, 1 - u, j + 1)
                        if j == 3 and has(b + 2):
                            c_split(b + 2, u, 0)
                    if g == 3 and has(b + 1):
                        c_pad(b + 1, j)
                    if has(b - 2):
                        if (j, g) == (0, 2):
                            c_z(b - 2)
                        if (j, g) == (0, 3):
                            c_stats(1, b - 2, z1, z1_ready)
                        if (j, g) == (1, 1):
                            if not (whole(b) and b == 2):
                                nc.vector.wait_ge(out_stored, 16 * (b - 2))
                            c_norm(1, b - 2, z1, res, res_ready)
                    if has(b - 1):
                        if (j, g) == (1, 1):
                            c_an(b - 1, 0)
                        if (j, g) == (1, 3):
                            c_an(b - 1, 1)
                        if (j, g) == (2, 3):
                            c_y3(b - 1)
                        if (j, g) == (3, 0):
                            c_stats(0, b - 1, y3, y3_ready)
                        if (j, g) == (3, 2):
                            c_norm(0, b - 1, y3, x3s, x3_ready)

        def c_hi(b, u, j):
            po = nc.gpsimd
            n = 4 * b + j
            po.wait_ge(p_ready, 8 if whole(b) and b < 2 else 16 * (b // 2) + 5)
            if not (whole(b) and n < 2):
                po.wait_ge(split_ready, 2 * (n - 1))
            par = (b // 2) % 2
            po.tensor_tensor(qk_hi[j % 2][:].rearrange("p k q -> p (k q)"),
                             qk_st[:, bass.ds(par, 1), 4 * u + j].rearrange("p o k c i -> p (o k c i)"),
                             one[:, 0:1].broadcast_to([P, 2 * S]), ALU.mult).then_inc(hi_ready, 1)

        def c_rs(i, t):
            po = nc.gpsimd
            po.wait_ge(ln_mv_ready[i], TB * (t + 1))
            po.tensor_tensor(ln_ve[i][:, :], ln_mv[i][:, :, 1], eps[:, 0:TB], ALU.add).then_inc(ln_ve_ready[i], 1)
            po.wait_ge(ln_ve_ready[i], t + 1)
            po.tensor_tensor(ln_rs[i][:, :], ln_ve[i][:, :], minus_half[:, 0:TB], ALU.pow).then_inc(ln_rs_ready[i], 1)

        def c_xr3b(t):
            po = nc.gpsimd
            po.wait_ge(xr3_loaded, 16 * (t + 1))
            if not (whole(t) and t == 0):
                po.wait_ge(y3_ready, t)
            po.tensor_tensor(xr3b[:], xr3[:], c_bo[:].unsqueeze(1).broadcast_to([P, TB, D]),
                             ALU.add).then_inc(xr3b_ready, 1)

        def c_x3b(t):
            po = nc.gpsimd
            po.wait_ge(x3_ready, TB * (t + 1))
            if not (whole(t) and t == 0):
                po.wait_ge(z1_ready, t)
            po.tensor_tensor(x3b[:], x3s[:], c_fb[:].unsqueeze(1).broadcast_to([P, TB, D]),
                             ALU.add).then_inc(x3b_ready, 1)

        def c_pool(b, u, p):
            for j in range(4):
                if j == 3 and has(b - 1):
                    c_rs(0, b - 1)
                if j < 2 and has(b + 1):
                    c_hi(b + 1, 1 - u, j + 2)
                if j >= 2 and has(b + 2):
                    c_hi(b + 2, u, j - 2)
                if j == 0 and has(b - 2):
                    c_rs(1, b - 2)
                if j == 1 and has(b - 1):
                    c_xr3b(b - 1)
                if j == 3 and has(b - 1):
                    c_x3b(b - 1)

        def c_load_kv(p):
            if not (whole(p) and p < 1):
                nc.sync.wait_ge(p_done, use(p - 2, 1, 7))
            nc.sync.dma_start(x_kv[:, :], x2T_d[:, bass.ds(p * 2 * S, 2 * S)]).then_inc(x_kv_loaded, 16)

        def c_load_q(p):
            if not (whole(p) and p < 1):
                nc.sync.wait_ge(p_done, 4 if whole(p) and p == 1 else use(p - 3, 1, 8))
            nc.sync.dma_start(x_q[:, :], x2T_d[:, bass.ds(p * 2 * S, 2 * S)]).then_inc(x_q_loaded, 16)

        def c_load_res(t):
            if not (whole(t) and t == 0):
                nc.sync.wait_ge(xr3b_ready, t)
            nc.sync.dma_start(xr3[:], x2_d.rearrange("(n p) d -> p n d", p=P)[:, bass.ds(t * TB, TB), :]
                              ).then_inc(xr3_loaded, 16)

        def c_store(t):
            nc.sync.wait_ge(res_ready, TB * (t + 1))
            nc.sync.dma_start(t_out.rearrange("(n p) d -> p n d", p=P)[:, bass.ds(t * TB, TB), :],
                              res[:]).then_inc(out_stored, 16)

        def c_k_alone(b, u, j):
            nc.sync.wait_ge(split_ready, 2 * (4 * b + j + 1))
            for g in range(GRP):
                lo = W32 * g
                nc.sync.dma_start(k_alone[u][lo:lo + W32, j, g, :].bitcast(FP32),
                                  k_m[u][lo:lo + W32, j, :].bitcast(FP32)).then_inc(k_alone_ready[j], 16)

        def c_sp(b, u, p):
            if has(b + 1):
                c_k_alone(b + 1, 1 - u, 1)
            if has(b - 1):
                c_load_res(b - 1)
            if u == 0 and wanted(p, "q", 2):
                c_load_q(p + 2)
            if has(b + 1):
                c_k_alone(b + 1, 1 - u, 2)
            if has(b - 2):
                c_store(b - 2)
            if has(b + 1):
                c_k_alone(b + 1, 1 - u, 3)
            if has(b + 2):
                c_k_alone(b + 2, u, 0)
            if u == 1 and wanted(p, "v", 2):
                c_load_kv(p + 2)

        def c_load_early():
            sp = nc.sync
            sp.wait_ge(d_done, (NTILE - 1) * NC + C_FREE)
            sp.dma_start(c_early[:, :], t["c_early"]).then_inc(c_loaded, 16)
            sp.dma_start(c_late[:].rearrange("p i d -> p (i d)"), t["c_late"]).then_inc(c_loaded, 16)
            sp.wait_ge(x2T_stored, 16 * (NTILE - 1))
            c_load_q(0)
            c_load_kv(0)

        C_FREE = -(-(C_EARLY + 5 * D + 6 * CH * W32 + 7 * CH + W32 + 1 + D + 4 * S) // (3 * P))

        def c_prepare():
            v = nc.vector
            v.wait_ge(c_loaded, 32)
            v.tensor_tensor(c_sins[:], c_sin[:], c_sgn[:], ALU.mult).then_inc(c_prep, 1)
            v.tensor_tensor(c_sinsp[:], c_sinp[:], c_sgnp[:], ALU.mult).then_inc(c_prep, 1)
            v.tensor_scalar(c_scale[:], c_scb[:], 1.0 / 127.0, None, ALU.mult).then_inc(c_prep, 1)
            v.wait_ge(c_prep, 3)
            wide = lambda a: a[:].unsqueeze(1).broadcast_to([P, CH, W32])
            for k in range(2):
                v.tensor_tensor(c_wt[2 * k][:], c_w[k][:], wide(c_cos), ALU.mult).then_inc(c_prep, 1)
                v.tensor_tensor(c_wt[2 * k + 1][:], c_ws[k][:], wide(c_sins), ALU.mult).then_inc(c_prep, 1)
                v.tensor_scalar(c_bt[:, 2 * k], c_b[:, k], c_cosp[:, 0:1], None, ALU.mult).then_inc(c_prep, 1)
                v.tensor_scalar(c_bt[:, 2 * k + 1], c_bs[:, k], c_sinsp[:, 0:1], None, ALU.mult).then_inc(c_prep, 1)
            v.wait_ge(c_prep, 11)
            for k in range(2):
                v.tensor_tensor(c_wr[k][:], c_wt[2 * k][:], c_wt[2 * k + 1][:], ALU.add).then_inc(c_prep, 1)
                v.scalar_tensor_tensor(c_br[:, k], c_bt[:, 2 * k], c_spec[:, k:k + 1], c_bt[:, 2 * k + 1],
                                       ALU.add, ALU.add).then_inc(c_prep, 1)
            v.tensor_scalar(c_br[:, 2], c_b[:, 2], c_spec[:, 2:3], None, ALU.add).then_inc(c_prep, 1)

        def c_zeros(i):
            nc.vector.memset(k_alone[i][:].bitcast(FP32), 0.0).then_inc(alone_zeroed, 1)

        C_PREP = 16

        def c_loop(eng, body):
            body(-1, 1, -1)
            body(0, 0, 0)
            body(1, 1, 0)
            with eng.Fori(1, NPAIR - 2) as p:
                body(p * 2, 0, p)
                body(p * 2 + 1, 1, p)
            for p in range(NPAIR - 2, NPAIR + 1):
                for u in range(2):
                    body(2 * p + u, u, p)

        def load_b_weights(c, n, n_select, c_select=None):
            if c_select is None:
                c_select = {0: 0, 4: 3}[c]
            w = t["w_all"].rearrange("p (c a m) -> p c a m", a=3, m=P)
            nc.gpsimd.dma_start(w_hi[:, bass.ds(c, n)], w[:, bass.ds(c, n)]).then_inc(w_hi_loaded, 16)
            s = t["select"].rearrange("p (c m) -> p c m", m=P)
            nc.gpsimd.dma_start(select[:, bass.ds(c_select, n_select)],
                                s[:, bass.ds(c_select, n_select)]).then_inc(w_hi_loaded, 16)

        B_LOADS = 2 * (NB - 1)
        assert 7 + 3 * (NB - 3) == NC and 5 + 3 * (NB - 3) == NCR

        @block.sync
        def _(sp):
            a_load_x(0)
            for k, name in ((2, "wvT"), (0, "wqT"), (1, "wkT")):
                sp.dma_start(a_w[k], t[name]).then_inc(w_loaded[k], 16)
            for dst, src in [(qb, t["qbT"]), (kb_, t["kbT"]), (vb, t["vb"].broadcast_to([P, H0 * P0]))]:
                sp.dma_start(dst[:], src).then_inc(early_consts, 16)
            a_copy_x(0)
            for dst, src in [(lb, t["lb"].broadcast_to([P, D])), (gate_b, t["gate_b"].broadcast_to([P, E])),
                             (gate_w, t["gate_wT"]), (tri, t["tri"].unsqueeze(0).broadcast_to([P, NG, NG])),
                             (ident, t["ident"]), (lw, t["lwT"].rearrange("(j p) d -> p j d", p=P))]:
                sp.dma_start(dst[:], src).then_inc(consts, 16)
            x_t = t["x"].rearrange("(n p) d -> p n d", p=P)
            sp.dma_start(xr[:], x_t[:, 0:TB, :]).then_inc(xr_loaded, 16)
            a_sp_batch(0, True, True, False)
            a_sp_batch(1, False, True, False)
            with sp.Fori(2, NB - 1) as b:
                a_sp_batch(b, False, False, False)
            a_sp_batch(NB - 1, False, False, True)
            sp.wait_ge(x1T_stored, 16 * (NB - 1))
            sp.wait_ge(x1_stored, 16 * (NB - 1))
            sp.wait_ge(rwT_stored, 16 * (NB - 2))
            b_load(0, 0)
            b_raw(0)
            b_raw(1)
            b_load_res(0)
            a_store_x1(NB - 1)
            a_store_rwT(NB - 2)
            a_store_rwT(NB - 1)
            b_sp()
            c_load_early()
            b_store(NTILE - 1)
            c_load_q(1)
            sp.wait_ge(alone_zeroed, 1)
            c_k_alone(0, 0, 0)
            sp.wait_ge(alone_zeroed, 2)
            c_loop(sp, c_sp)
            sp.wait_ge(out_stored, 16 * NB)

        @block.tensor
        def _(pe):
            pe.wait_ge(a_w_lo_ready, 1)
            a_v_part(0, 0, 0)
            pe.wait_ge(a_w_lo_ready, 3)
            a_qk(0, 0)
            a_v_part(0, 0, 1)
            a_qk(0, 1)
            a_scores(0, 0)
            pe.wait_ge(consts, 16 * 6)
            a_pe_batch(0, True, True, False)
            a_pe_batch(1, False, True, False)
            with pe.Fori(2, NB - 1) as b:
                a_pe_batch(b, False, False, False)
            a_pe_batch(NB - 1, False, False, True)
            a_pv(NB - 1, NJ - 1)
            a_out(NB - 1)
            a_x1T(NB - 1)
            a_logits(NB - 1)
            a_rwT(NB - 2, 4 * NB, NB)
            a_rwT(NB - 1, 4 * NB, NB)
            pe.wait_ge(rwT_ready, NB)
            pe.wait_ge(w_hi_loaded, 16 * B_LOADS)
            b_pe_tile(0, 0, True)
            with pe.Fori(0, NTILE // 2 - 1) as k:
                n = k * 2 + 1
                b_pe_tile(n, 1, False)
                b_pe_tile(n + 1, 0, False)
            b_pe_tile(NTILE - 1, 1, False)
            b_down(NTILE - 1, NC - 2)
            b_down(NTILE - 1, NC - 1)
            b_oT(NTILE - 1)
            pe.wait_ge(c_prep, C_PREP)
            pe.wait_ge(hf_ready, NTILE * NCR)
            for n, (what, part, ahead) in enumerate(START):
                if n == 5:
                    b_x2T(NTILE - 1)
                c_project(-1, what, part, n, ahead, True)
            pe.wait_ge(x2T_ready, NTILE)
            c_loop(pe, c_pe)

        @block.scalar
        def _(act):
            for k, scale in ((2, 1.0), (0, 0.125), (1, 1.0)):
                act.wait_ge(w_loaded[k], 16)
                act.mul(a_w_hi[k][:, :], a_w[k], scale).then_inc(a_w_hi_ready, 1)
            act.wait_ge(early_consts, 16 * 3)
            act.mul(qb8[:, :], qb[:, :], 0.125).then_inc(qb8_ready, 1)
            act.wait_ge(qb8_ready, 1)
            a_qk_out(0, 0)
            a_qk_out(0, 1)
            a_exp(0, 0, 0)
            a_exp(0, 0, 1)
            a_act_batch(0, True, True, False)
            a_act_batch(1, False, True, False)
            with act.Fori(2, NB - 1) as b:
                a_act_batch(b, False, False, False)
            a_act_batch(NB - 1, False, False, True)
            a_c_out(NB - 1, NJ - 1)
            a_x1T_out(NB - 1)
            a_r_exp(NB - 1)
            a_rwT_out(NB - 2)
            a_rwT_out(NB - 1)
            act.wait_ge(rwT_stored, 16 * NB)
            b_x_hi(0, 0)
            b_act_tile(0, 0, True, False)
            with act.Fori(0, NTILE // 2 - 1) as k:
                n = k * 2 + 1
                b_act_tile(n, 1, False, False)
                b_act_tile(n + 1, 0, False, False)
            b_act_tile(NTILE - 1, 1, False, True)
            b_h_hi(NTILE - 1, NC - 1)
            b_oT_out(NTILE - 1)
            act.wait_ge(c_prep, C_PREP)
            for n, (what, part, ahead) in enumerate(START):
                if n == 5:
                    b_x2T_out(NTILE - 1)
                c_project_out(-1, 0, what, part, n, ahead, True)
            c_loop(act, c_act)

        @block.vector
        def _(dve):
            for n, (k, scale) in enumerate(((2, 1.0), (0, 0.125), (1, 1.0))):
                dve.wait_ge(a_w_hi_ready, n + 1)
                dve.scalar_tensor_tensor(a_w_lo[k][:, :], a_w[k], scale, a_w_hi[k][:, :].bitcast(FP32),
                                         ALU.mult, ALU.subtract).then_inc(a_w_lo_ready, 1)
            dve.wait_ge(early_consts, 16 * 3)
            dve.wait_ge(qb8_ready, 1)
            a_v_out(0, 0, 0)
            a_qk_lo(0, 0)
            a_v_out(0, 0, 1)
            a_qk_lo(0, 1)
            a_max(0, 0)
            dve.wait_ge(consts, 16 * 6)
            a_dve_batch(0, True, True, False)
            a_dve_batch(1, False, True, False)
            with dve.Fori(2, NB - 1) as b:
                a_dve_batch(b, False, False, False)
            a_dve_batch(NB - 1, False, False, True)
            route_groups(NB - 2)
            route_best_eight(NB - 2)
            route_weights(NB - 2)
            a_y(NB - 1)
            a_stats(NB - 1)
            a_norm(NB - 1)
            route_scores(NB - 1)
            route_best_two(NB - 1)
            route_groups(NB - 1)
            route_best_eight(NB - 1)
            route_weights(NB - 1)
            dve.wait_ge(rwT_stored, 16 * NB)
            dve.wait_ge(w_hi_loaded, 16 * B_LOADS)
            b_lo(0)
            b_lo(1)
            b_dve_tile(0, True)
            with dve.Fori(0, NTILE // 2 - 1) as k:
                n = k * 2 + 1
                b_dve_tile(n, False)
                b_dve_tile(n + 1, False)
            b_dve_tile(NTILE - 1, False)
            c_prepare()
            b_y(NTILE - 1)
            b_stats(NTILE - 1)
            b_mv(NTILE - 1)
            b_norm(NTILE - 1, range(SUB))
            dve.wait_ge(d_done, NTILE * NC)
            dve.memset(mx_pad[:], 0.0).then_inc(pad_ready, 1)
            c_zeros(0)
            dve.wait_ge(x2_stored, 16 * NTILE)
            dve.wait_ge(x2T_stored, 16 * NTILE)
            c_split(0, 0, 0)
            c_zeros(1)
            c_loop(dve, c_dve)

        @block.gpsimd
        def _(pool):
            pool.memset(minus_half[:, :], -0.5).then_inc(const_ready, 1)
            pool.memset(eps[:, :], EPS).then_inc(const_ready, 1)
            pool.memset(one[:, :], 1.0).then_inc(const_ready, 1)
            pool.wait_ge(const_ready, 3)
            a_x_half(0)
            pool.wait_ge(consts, 16 * 6)
            a_pool_batch(0, True, True, False)
            load_b_weights(0, 4, 3)
            a_pool_batch(1, False, True, False)
            load_b_weights(4, 3, 2)
            with pool.Fori(2, NB - 1) as b:
                a_pool_batch(b, False, False, False)
                load_b_weights((b - 2) * 3 + 7, 3, 3, (b - 2) * 3 + 5)
            a_pool_batch(NB - 1, False, False, True)
            a_rstd(NB - 1)
            pool.wait_ge(rwT_stored, 16 * NB)
            b_x_lo(0, 0)
            b_pool_tile(0, 0, True, False)
            with pool.Fori(0, NTILE // 2 - 1) as k:
                n = k * 2 + 1
                b_pool_tile(n, 1, False, False)
                b_pool_tile(n + 1, 0, False, False)
            b_pool_tile(NTILE - 1, 1, False, True)
            b_rstd(NTILE - 1)
            c_hi(0, 0, 0)
            c_hi(0, 0, 1)
            c_loop(pool, c_pool)


def blocks(routed, shared):
    import numpy as np
    pad = np.zeros((NC * P - FF, D), np.float32)
    return np.concatenate([routed.reshape(E * I, D), shared, pad]).reshape(NC, P, D)


def chunked(w, times):
    import numpy as np
    out = np.zeros((P, CH, W32), np.float32)
    for k in range(times):
        out[:, :, 9 * k + 1:9 * k + 9] = w.T.reshape(D, CH, D1)
    return out.reshape(P, CH * W32)


def chunked_bias(b, times):
    import numpy as np
    out = np.zeros((GRP, W32, CH), np.float32)
    for k in range(times):
        out[:, 9 * k + 1:9 * k + 9, :] = b.reshape(CH, D1).T
    return out.reshape(P, CH)


def tripled(v8):
    import numpy as np
    out = np.zeros(W32, np.float32)
    for k in range(3):
        out[9 * k + 1:9 * k + 9] = v8
    return out


def partner(a):
    return a.reshape(a.shape[0] // 2, 2, -1)[:, ::-1].reshape(a.shape)


def layout(v):
    import numpy as np
    x = v["L0_attn_x"].reshape(TOK, D)
    heads = lambda w: w.reshape(H0 * P0, D).T
    gate = blocks(v["L0_ffn_Wg"], v["L0_ffn_Sg"]).transpose(2, 0, 1)
    up = blocks(v["L0_ffn_Wu"], v["L0_ffn_Su"]).transpose(2, 0, 1)
    down = blocks(v["L0_ffn_Wd"].transpose(0, 2, 1), v["L0_ffn_Sd"].T).transpose(1, 0, 2)
    belongs = (np.arange(E * I)[None] // I == np.arange(E)[:, None]).astype(np.float32)
    wq, wk, wv, bq, bk, bv = (v["L1_attn_" + n] for n in ("wq", "wk", "wv", "bq", "bk", "bv"))
    cos = tripled(np.repeat(v["L1_attn_rot_cos"][S], 2))
    sin = tripled(np.repeat(v["L1_attn_rot_sin"][S], 2))
    sign = tripled(np.tile(np.float32([-1, 1]), D1 // 2))
    spec = np.zeros((GRP, W32, 3), np.float32)
    spec[:, 0:19:9, 1] = -1
    spec[:, 0, 2] = 1
    low = np.zeros((GRP, W32, 2), np.float32)
    low[:, 9:18, 0] = -1
    low[:, 18:27, 1] = -1
    wide = lambda row: np.broadcast_to(row[None], (P, row.size))
    early = [chunked(wq, 3), chunked(wk, 3), chunked(wv, 1), chunked(partner(wq), 3), chunked(partner(wk), 3),
             chunked_bias(bq, 3), chunked_bias(bk, 3), chunked_bias(bv, 1),
             chunked_bias(partner(bq), 3), chunked_bias(partner(bk), 3), wide(cos), wide(sin), wide(sign),
             np.tile(cos, GRP)[:, None], np.tile(sin, GRP)[:, None], np.tile(sign, GRP)[:, None],
             spec.reshape(P, 3), low.reshape(P, 2)]
    rows = np.concatenate([wide(v["L1_attn_bo"]), wide(v["L1_ffn_SCB"]), wide(v["L1_ffn_bias"])], 1)
    return dict(
        x=x, xT=x.T, wqT=heads(v["L0_attn_q_w"]), wkT=heads(v["L0_attn_k_w"]), wvT=heads(v["L0_attn_v_w"]),
        qbT=v["L0_attn_q_b"].reshape(NJ, P).T, kbT=v["L0_attn_k_b"].reshape(NJ, P).T,
        vb=v["L0_attn_v_b"].reshape(1, H0 * P0), lb=v["L0_attn_l_b"].reshape(1, D), lwT=v["L0_attn_l_w"].T,
        gate_b=v["L0_ffn_gate_bias"].reshape(1, E), gate_wT=v["L0_ffn_gate_w"].T,
        tri=np.tril(np.ones((NG, NG), np.float32), -1), ident=np.eye(P, dtype=np.float32),
        w_all=np.stack([gate, up, down], 2).reshape(P, NC * 3 * P), select=np.concatenate([belongs, belongs]),
        c_early=np.concatenate(early, 1), c_late=np.concatenate([v["L1_attn_wo"].T, v["L1_ffn_CB"].T, rows], 1))


def kernel(**inputs):
    import numpy as np
    from concourse import bacc
    from concourse.bass_utils import run_bass_kernel_spmd

    nc = bacc.Bacc("TRN2", target_bir_lowering=False, num_devices=1)
    laid = {k: np.ascontiguousarray(a) for k, a in layout({k: np.asarray(a) for k, a in inputs.items()}).items()}
    t = {k: nc.dram_tensor(f"in_{k}_dram", a.shape, mybir.dt.from_np(a.dtype), kind="ExternalInput").ap()
         for k, a in laid.items()}
    t["out"] = nc.dram_tensor("out_0_dram", (TOK, D), FP32, kind="ExternalOutput").ap()
    build(nc, t)
    result = run_bass_kernel_spmd(nc, [{f"in_{k}_dram": a for k, a in laid.items()}], core_ids=[0])
    return result.results[0]["out_0_dram"].reshape(NB, S, D)
```
